# Optimizing a Trainium2 kernel written in Bass

```python
import numpy as np
import jax
import jax.numpy as jnp

def _softmax(x, axis=-1):
    return jax.nn.softmax(x, axis=axis)
def _gelu(x):
    return jax.nn.gelu(x, approximate=True)
def _silu(x):
    return jax.nn.silu(x)
def _sigmoid(x):
    return jax.nn.sigmoid(x)
def _layernorm(x, axis=-1, eps=1e-5):
    m = jnp.mean(x, axis=axis, keepdims=True)
    v = jnp.var(x, axis=axis, keepdims=True)
    return (x - m) / jnp.sqrt(v + eps)
def _scatter_add(tgt, idx, src, axis=0):
    return tgt.at[idx].add(src)
def _segment_sum(src, seg, n):
    return jax.ops.segment_sum(src, seg, n)

kernel_name = 'mk_adj_resnorm_d2_adj_128_d0952c'

def setup_inputs(seed: int = 0):
    np.random.seed(seed)
    _w = jnp.asarray
    def _rec_inputs():
        import jax
        import jax.numpy as jnp
        _gk = jax.random.key(seed)
        x = 0.0002279 + 0.9999 * jax.random.normal(jax.random.fold_in(_gk, 1), (8192, 128), jnp.float32)
        _a = jax.random.bernoulli(jax.random.fold_in(_gk, 2), 0.00390625, (8192, 8192))
        _a = jnp.logical_or(_a, jnp.swapaxes(_a, -1, -2))
        _a = jnp.logical_or(_a, jnp.eye(8192, dtype=bool))
        adj = _a.astype(jnp.int32)
        return x, adj
    x, adj = _rec_inputs()
    def _L0_gnn_setup():
        import jax, jax.numpy as jnp
        import numpy as np
        N = 8192
        F_IN = 128
        D = 128
        NEG_SLOPE = 0.2
        MASK_FILL = -9000000000000000.0
        key = jax.random.key(seed)
        k1, k2, k3, k4 = jax.random.split(key, 4)
        A = jax.random.randint(k1, (N, N), 0, 2, dtype=jnp.int32)
        X = jax.random.normal(k2, (N, F_IN), dtype=jnp.float32)
        lim_w = float(np.sqrt(6.0 / (F_IN + D)))
        Ws = jax.random.uniform(k3, (F_IN, D), minval=-lim_w, maxval=lim_w, dtype=jnp.float32)
        lim_a = 1.414 * float(np.sqrt(6.0 / (2 * D + 1)))
        a = jax.random.uniform(k4, (2 * D, 1), minval=-lim_a, maxval=lim_a, dtype=jnp.float32)
        return {'A': A, 'X': X, 'Ws': Ws, 'a': a}
    _L0_gnn_all = _L0_gnn_setup()
    _L0_gnn_in = {k: v for k, v in _L0_gnn_all.items() if k in ('Ws', 'a', )}
    del _L0_gnn_all

    def _L1_gnn_setup():
        import jax, jax.numpy as jnp
        import numpy as np
        N, IN_DIM, OUT_DIM, H = (4096, 128, 128, 4)
        HEAD_DIM = OUT_DIM // H
        NEG_SLOPE = 0.2
        key = jax.random.key(seed)
        k1, k2, k3, k4, k5 = jax.random.split(key, 5)
        x = jax.random.normal(k1, (N, IN_DIM), dtype=jnp.float32)
        adj = jax.random.randint(k2, (N, N), 0, 2, dtype=jnp.int32)
        W = jax.random.normal(k3, (OUT_DIM, IN_DIM), dtype=jnp.float32) * (1.0 / np.sqrt(IN_DIM))
        attn_src = jax.random.normal(k4, (1, H, HEAD_DIM), dtype=jnp.float32) * 0.1
        attn_dst = jax.random.normal(k5, (1, H, HEAD_DIM), dtype=jnp.float32) * 0.1
        return {'x': x, 'adj': adj, 'W': W, 'attn_src': attn_src, 'attn_dst': attn_dst}
    _L1_gnn_all = _L1_gnn_setup()
    _L1_gnn_in = {k: v for k, v in _L1_gnn_all.items() if k in ('W', 'attn_src', 'attn_dst', )}
    del _L1_gnn_all

    return {
        "x": x,
        "adj": adj,
        "L0_gnn_Ws": _L0_gnn_in["Ws"],
        "L0_gnn_a": _L0_gnn_in["a"],
        "L1_gnn_W": _L1_gnn_in["W"],
        "L1_gnn_attn_src": _L1_gnn_in["attn_src"],
        "L1_gnn_attn_dst": _L1_gnn_in["attn_dst"],
    }

def reference(x, adj, L0_gnn_Ws, L0_gnn_a, L1_gnn_W, L1_gnn_attn_src, L1_gnn_attn_dst):
    import jax
    import jax.numpy as jnp
    def _L0_gnn_ref(A, X, Ws, a):
        import jax, jax.numpy as jnp
        import numpy as np
        N = 8192
        F_IN = 128
        D = 128
        NEG_SLOPE = 0.2
        MASK_FILL = -9000000000000000.0
        Wh = X @ Ws
        d = Wh.shape[-1]
        e1 = Wh @ a[:d]
        e2 = Wh @ a[d:]
        e = jax.nn.leaky_relu(e1 + e2.T, negative_slope=NEG_SLOPE)
        e = jnp.where(A > 0, e, MASK_FILL)
        attn = jax.nn.softmax(e, axis=1)
        H = attn @ Wh
        return H

    def _L1_gnn_ref(x, adj, W, attn_src, attn_dst):
        import jax, jax.numpy as jnp
        import numpy as np
        N, IN_DIM, OUT_DIM, H = (4096, 128, 128, 4)
        HEAD_DIM = OUT_DIM // H
        NEG_SLOPE = 0.2
        n = x.shape[0]
        h = (x @ W.T).reshape(n, H, HEAD_DIM)
        e_src = jnp.sum(h * attn_src, axis=-1)
        e_dst = jnp.sum(h * attn_dst, axis=-1)
        e = e_src[:, None, :] + e_dst[None, :, :]
        e = jax.nn.leaky_relu(e, negative_slope=NEG_SLOPE)
        e = jnp.where((adj == 0)[:, :, None], -jnp.inf, e)
        alpha = jax.nn.softmax(e, axis=1)
        out = jnp.einsum('ijh,jhd->ihd', alpha, h)
        return out.reshape(n, -1)

    x = _layernorm(x + _L0_gnn_ref(adj, x, L0_gnn_Ws, L0_gnn_a), axis=-1)
    x = _layernorm(x + _L1_gnn_ref(x, adj, L1_gnn_W, L1_gnn_attn_src, L1_gnn_attn_dst), axis=-1)
    return x


_drawn_inputs = setup_inputs


def setup_inputs(seed=0):
    import zlib

    import numpy as np

    out = dict(_drawn_inputs(seed))
    spreads = {}
    factors = {}
    for name, (base, spread) in spreads.items():
        noise = np.random.default_rng([zlib.crc32(name.encode()), seed]).standard_normal(out[name].shape)
        drawn = base * np.exp(spread * noise) if base else spread * noise
        out[name] = jnp.asarray(drawn.astype(out[name].dtype))
    for name, factor in factors.items():
        out[name] = (out[name] * factor).astype(out[name].dtype)
    return out
```

```python
from contextlib import ExitStack

import concourse.bass as bass
from concourse import mybir

FP32, BF16, I8, I32, FP8 = (mybir.dt.float32, mybir.dt.bfloat16, mybir.dt.int8, mybir.dt.int32,
                            mybir.dt.float8e4)
ALU = mybir.AluOpType
ACT = mybir.ActivationFunctionType
AX = mybir.AxisListType

P = 128
JB = 4
IT = 4
SLAB = IT * P
PARTS = 3
BRANCHES = 2
ON = 64.0
SLOPE = 0.2
EPS = 1e-5
ADJ_SLOTS = 4
OUT_SLOTS = 4
EDGE_SLOTS = 4
MASK_SLOTS = 2
SCALAR_SHARE = (0, 1, 3, 4, 6, 8, 9, 11, 12, 14)


class Layer:

    def __init__(self, index, heads):
        self.index, self.heads = index, heads
        self.width = P // heads + 1
        self.head_cols = PARTS * self.width


def chain(eng, sem):
    count = [0]

    def link(instruction):
        count[0] += 1
        instruction.then_inc(sem, 1)
        eng.wait_ge(sem, count[0])

    return link


def stand(wait, passed):
    wait.then_inc(passed, 1)


def project(nc, keep, L, x_dram, feat_t_dram, proj, proj_t, att, score_row_dram, parts, cols, n):
    H, W = L.heads, L.width
    tiles = n // P
    groups = tiles // JB
    gw = JB * P
    name = f"l{L.index}_"
    with ExitStack() as ctx:
        sb = lambda s, shape, dt: ctx.enter_context(nc.sbuf_tensor(name + s, shape, dt))
        pb = lambda s, shape, dt: ctx.enter_context(nc.psum_tensor(name + s, shape, dt))
        sem = lambda s: keep.enter_context(nc.semaphore(name + s))

        feat_t = sb("feat_t", [P, n], FP32)
        feat = sb("feat", [P, tiles, P], FP32) if x_dram is not None else None
        ident = sb("ident", [P, P], FP32)
        proj_sb = sb("proj_sb", [P, P], FP32)
        proj_t_sb = sb("proj_t_sb", [P, P], FP32)
        att_sb = sb("att_sb", [P, 2 * H], FP32)
        watt = sb("watt", [P, 2 * H], FP32)
        scores = sb("scores", [P, tiles, 2 * H], FP32)
        pmax = sb("pmax", [P, H], FP32)
        gmax = sb("gmax", [P, H], FP32)
        z1 = sb("z1", [P, tiles, H], FP32)
        z2 = sb("z2", [P, tiles, H], FP32)
        z_alpha = sb("z_alpha", [P, tiles, H], FP32)
        z_beta = sb("z_beta", [P, tiles, H], FP32)
        wgt = sb("wgt", [P, BRANCHES, tiles, H], FP32)
        vals = sb("vals", [P, 2, JB * H, W], FP32)
        full = sb("full", [P, BRANCHES, JB * H, W], FP32)
        rest = sb("rest", [P, BRANCHES, JB * H, W], FP32)
        row_sb = parts[0:H, 0:2 * n].bitcast(FP32)

        tr_ps = [pb(f"tr_ps{i}", [P, gw], FP32) for i in range(2)]
        row_ps = [pb(f"row_ps{i}", [P, gw], FP32) for i in range(2)]
        val_ps = [pb(f"val_ps{i}", [P, gw], FP32) for i in range(2)]
        score_ps = pb("score_ps", [P, 512], FP32)
        watt_ps = pb("watt_ps", [P, 2 * H], FP32)

        weights_in, att_zero = sem("weights_in"), sem("att_zero")
        feat_in = [sem(f"feat_in{g}") for g in range(groups)]
        ident_zero, ident_ready = sem("ident_zero"), sem("ident_ready")
        watt_done, watt_ready = sem("watt_done"), sem("watt_ready")
        tr_done, feat_t_ready = sem("tr_done"), sem("feat_t_ready")
        row_done, row_ready, row_stored = sem("row_done"), sem("row_ready"), sem("row_stored")
        scores_done, scores_ready = sem("scores_done"), sem("scores_ready")
        pmax_ready, gmax_ready = sem("pmax_ready"), sem("gmax_ready")
        expo_ready, expo_done, dve_seq = sem("expo_ready"), sem("expo_done"), sem("dve_seq")
        ones_ready = sem("ones_ready")
        val_done, val_ready = sem("val_done"), sem("val_ready")
        full_ready, hi_ready = sem("full_ready"), sem("hi_ready")
        rest_ready, mid_ready, lo_ready = sem("rest_ready"), sem("mid_ready"), sem("lo_ready")

        pv = parts[:, 0:BRANCHES * tiles * H * PARTS * W].rearrange(
            "p (b g k w) -> p b g k w", b=BRANCHES, k=PARTS, w=W)
        n_weights = 2 if H == 1 else 2 + 2 * H
        block = ctx.enter_context(nc.Block())

        @block.sync
        def _(sp):
            sp.dma_start(proj_sb[:, :], proj).then_inc(weights_in, 16)
            sp.dma_start(proj_t_sb[:, :], proj_t).then_inc(weights_in, 16)
            if H == 1:
                sp.dma_start(att_sb[:, :], att[0]).then_inc(att_zero, 16)
            else:
                sp.wait_ge(att_zero, 1)
                for k in range(2):
                    for h in range(H):
                        d = P // H
                        sp.dma_start(att_sb[h * d:(h + 1) * d, k * H + h:k * H + h + 1],
                                     att[k][h]).then_inc(weights_in, 16)
            for g in range(groups):
                if feat is not None:
                    sp.dma_start(feat[:, g * JB:(g + 1) * JB, :],
                                 x_dram[g * gw:(g + 1) * gw, :].rearrange("(t p) d -> p t d", p=P)
                                 ).then_inc(feat_in[g], 16)
                elif g % JB == 0:
                    sp.dma_start(feat_t[:, g * gw:(g + JB) * gw],
                                 feat_t_dram[:, g * gw:(g + JB) * gw]).then_inc(feat_in[g], 16)
            sp.wait_ge(row_ready, groups)
            sp.dma_start(score_row_dram, row_sb).then_inc(row_stored, 16)
            sp.wait_ge(row_stored, 16)

        @block.gpsimd
        def _(pool):
            if feat is not None:
                nc.gpsimd.memset(ident[:, :], 0.0).then_inc(ident_zero, 1)
                pool.wait_ge(ident_zero, 1)
                nc.gpsimd.affine_select(out=ident[:, :], in_=ident[:, :], compare_op=ALU.not_equal,
                                        fill=1.0, base=0, pattern=[[-1, P]],
                                        channel_multiplier=1).then_inc(ident_ready, 1)
            pool.wait_ge(pmax_ready, 1)
            nc.gpsimd.partition_all_reduce(gmax[:, :], pmax[:, :], P,
                                           bass.bass_isa.ReduceOp.max).then_inc(gmax_ready, 1)
            for g in range(groups):
                for b in range(BRANCHES):
                    pool.wait_ge(mid_ready, BRANCHES * g + b + 1)
                    nc.gpsimd.tensor_tensor(pv[:, b, g * JB * H:(g + 1) * JB * H, 2, :],
                                            rest[:, b, :, :],
                                            pv[:, b, g * JB * H:(g + 1) * JB * H, 1, :],
                                            ALU.subtract).then_inc(lo_ready, 1)

        @block.tensor
        def _(pe):
            pe.wait_ge(weights_in, 16 * n_weights)
            if H == 1:
                pe.wait_ge(att_zero, 16)
            nc.tensor.matmul(watt_ps[:, :], proj_t_sb[:, :], att_sb[:, :], start=True,
                             stop=True).then_inc(watt_done, 1)
            if feat is not None:
                pe.wait_ge(ident_ready, 1)
            pe.wait_ge(watt_ready, 1)

            def transpose(g):
                pe.wait_ge(feat_in[g], 16)
                if g >= 2:
                    pe.wait_ge(feat_t_ready, g - 1)
                for t in range(JB):
                    last = nc.tensor.transpose(tr_ps[g % 2][:, t * P:(t + 1) * P],
                                               feat[:, g * JB + t, :], ident[:, :])
                last.then_inc(tr_done, 1)

            if feat is not None:
                transpose(0)
            for g in range(groups):
                if feat is not None:
                    if g + 1 < groups:
                        transpose(g + 1)
                    pe.wait_ge(feat_t_ready, g + 1)
                else:
                    pe.wait_ge(feat_in[g // JB * JB], 16)
                if g >= 2:
                    pe.wait_ge(row_ready, g - 1)
                nc.tensor.matmul(row_ps[g % 2][0:H, :], watt[:, 0:H], feat_t[:, g * gw:(g + 1) * gw],
                                 start=True, stop=True).then_inc(row_done, 1)
                for t in range(g * JB, (g + 1) * JB):
                    last = nc.tensor.matmul(score_ps[:, t * 2 * H:(t + 1) * 2 * H],
                                            feat_t[:, t * P:(t + 1) * P], watt[:, :],
                                            start=True, stop=True)
            last.then_inc(scores_done, 1)
            for g in range(groups):
                if g >= 2:
                    pe.wait_ge(val_ready, g - 1)
                for t in range(JB):
                    last = nc.tensor.matmul(val_ps[g % 2][:, t * P:(t + 1) * P],
                                            feat_t[:, (g * JB + t) * P:(g * JB + t + 1) * P],
                                            proj_sb[:, :], start=True, stop=True)
                last.then_inc(val_done, 1)

        @block.scalar
        def _(act):
            for g in range(groups):
                act.wait_ge(row_done, g + 1)
                nc.scalar.activation(row_sb[:, g * gw:(g + 1) * gw], row_ps[g % 2][0:H, :],
                                     ACT.Copy).then_inc(row_ready, 1)
            act.wait_ge(row_stored, 16)
            act.wait_ge(expo_ready, 1)
            nc.scalar.activation(wgt[:, 0], z1[:, :, :], ACT.Exp)
            nc.scalar.activation(wgt[:, 1], z1[:, :, :], ACT.Exp, scale=SLOPE).then_inc(expo_done, 1)
            act.wait_ge(expo_ready, 2)
            nc.scalar.activation(cols["alpha"][:, :, :], z_alpha[:, :, :], ACT.Exp)
            nc.scalar.activation(cols["beta"][:, :, :], z_beta[:, :, :], ACT.Exp)

            def values(g):
                act.wait_ge(val_done, g + 1)
                if g >= 2:
                    act.wait_ge(full_ready, BRANCHES * (g - 1))
                nc.scalar.activation(
                    vals[:, g % 2, :, 0:W - 1],
                    val_ps[g % 2][:, :].rearrange("p (g w) -> p g w", w=W - 1),
                    ACT.Copy).then_inc(val_ready, 1)

            act.wait_ge(ones_ready, 1)
            values(0)
            for g in range(groups):
                if g + 1 < groups:
                    values(g + 1)
                for b in range(BRANCHES):
                    act.wait_ge(full_ready, BRANCHES * g + b + 1)
                    nc.scalar.activation(pv[:, b, g * JB * H:(g + 1) * JB * H, 0, :],
                                         full[:, b, :, :], ACT.Copy).then_inc(hi_ready, 1)
                for b in range(BRANCHES):
                    act.wait_ge(rest_ready, BRANCHES * g + b + 1)
                    nc.scalar.activation(pv[:, b, g * JB * H:(g + 1) * JB * H, 1, :],
                                         rest[:, b, :, :], ACT.Copy).then_inc(mid_ready, 1)

        @block.vector
        def _(dve):
            link = chain(dve, dve_seq)
            if H > 1:
                nc.vector.memset(att_sb[:, :], 0.0).then_inc(att_zero, 1)
            nc.vector.memset(vals[:, :, :, W - 1:W], 1.0).then_inc(ones_ready, 1)
            dve.wait_ge(watt_done, 1)
            nc.vector.tensor_copy(watt[:, :], watt_ps[:, :]).then_inc(watt_ready, 1)
            if feat is not None:
                for g in range(groups):
                    dve.wait_ge(tr_done, g + 1)
                    nc.vector.tensor_copy(feat_t[:, g * gw:(g + 1) * gw],
                                          tr_ps[g % 2][:, :]).then_inc(feat_t_ready, 1)
            dve.wait_ge(scores_done, 1)
            link(nc.vector.tensor_copy(scores[:, :, :].rearrange("p t c -> p (t c)"),
                                       score_ps[:, 0:tiles * 2 * H]))
            s_cols, t_cols = scores[:, :, 0:H], scores[:, :, H:2 * H]
            nc.vector.tensor_reduce(pmax[:, :], t_cols.rearrange("p t h -> p h t"), AX.X,
                                    ALU.max).then_inc(pmax_ready, 1)
            link(nc.vector.tensor_scalar(cols["t_neg"][:, :, :], t_cols, -1.0, None, ALU.mult))
            top = gmax[:, :].unsqueeze(1).broadcast_to([P, tiles, H])
            dve.wait_ge(gmax_ready, 1)
            nc.vector.tensor_tensor(z1[:, :, :], t_cols, top, ALU.subtract).then_inc(expo_ready, 1)
            link(nc.vector.tensor_tensor(z2[:, :, :], s_cols, top, ALU.add))
            nc.vector.tensor_scalar(z_alpha[:, :, :], z2[:, :, :], 1.0 - SLOPE, 0.0, ALU.mult,
                                    ALU.min)
            nc.vector.tensor_scalar(z_beta[:, :, :], z2[:, :, :], SLOPE - 1.0, 0.0, ALU.mult,
                                    ALU.min).then_inc(expo_ready, 1)
            dve.wait_ge(expo_done, 1)
            for g in range(groups):
                dve.wait_ge(val_ready, g + 1)
                for b in range(BRANCHES):
                    if g >= 1:
                        dve.wait_ge(hi_ready, BRANCHES * (g - 1) + b + 1)
                        dve.wait_ge(rest_ready, BRANCHES * (g - 1) + b + 1)
                    w = wgt[:, b, g * JB:(g + 1) * JB, :].rearrange("p t h -> p (t h)")
                    nc.vector.tensor_tensor(full[:, b, :, :], vals[:, g % 2, :, :],
                                            w.unsqueeze(2).broadcast_to([P, JB * H, W]),
                                            ALU.mult).then_inc(full_ready, 1)
                for b in range(BRANCHES):
                    dve.wait_ge(hi_ready, BRANCHES * g + b + 1)
                    if g >= 1:
                        dve.wait_ge(lo_ready, BRANCHES * (g - 1) + b + 1)
                    nc.vector.tensor_tensor(rest[:, b, :, :], full[:, b, :, :],
                                            pv[:, b, g * JB * H:(g + 1) * JB * H, 0, :],
                                            ALU.subtract).then_inc(rest_ready, 1)


def attend(nc, keep, L, adj, edge_bytes, x_dram, out_dram, score_row_dram, parts, cols, n, act_heads):
    H, W, HC = L.heads, L.width, L.head_cols
    tiles = n // P
    slabs = n // SLAB
    nb = tiles // JB
    ahead = max(1, nb // 2 - 1)
    words = JB * SLAB // 4
    first = L.index == 0
    name = f"l{L.index}_"
    G = IT * H
    with ExitStack() as ctx:
        sb = lambda s, shape, dt: ctx.enter_context(nc.sbuf_tensor(name + s, shape, dt))
        sem = lambda s: keep.enter_context(nc.semaphore(name + s))

        s_rows = sb("s_rows", [P, 2 * H * SLAB], FP32)
        above = [sb(f"above{i}", [P, H, JB * SLAB], I8) for i in range(MASK_SLOTS)]
        pos = [sb(f"pos{i}", [P, H, JB * SLAB], I8) for i in range(MASK_SLOTS)]
        neg = [sb(f"neg{i}", [P, H, JB * SLAB], I8) for i in range(MASK_SLOTS)]
        if first:
            adj_sb = [sb(f"adj_sb{i}", [P, JB * SLAB], I32) for i in range(ADJ_SLOTS)]
            edge = [sb(f"edge{i}", [P, JB * SLAB], I8) for i in range(MASK_SLOTS)]
            next_edge = [sb(f"next_edge{i}", [P, JB * SLAB], I8) for i in range(OUT_SLOTS)]
        else:
            edge = [sb(f"edge{i}", [P, JB * SLAB], I8) for i in range(EDGE_SLOTS)]
        sums = sb("sums", [P, IT, BRANCHES, H, PARTS, W], FP32)
        acc = [sb(f"acc{b}", [P, IT, H, W], FP32) for b in range(BRANCHES)]
        x_sb = sb("x_sb", [P, IT, P], FP32)
        y_sb = sb("y_sb", [P, IT, P], FP32)
        inv = sb("inv", [P, G], FP32)
        power = sb("power", [P, G], FP32)
        stats = sb("stats", [P, IT, 6], FP32)
        moments = sb("moments", [P, IT, 2], FP32)
        rstd = sb("rstd", [P, IT], FP32)
        half = sb("half", [P, IT], FP32)
        sum_ps = [[ctx.enter_context(nc.psum_tensor(f"{name}sum_ps{i}_{b}", [P, 512], FP32))
                   for b in range(BRANCHES)] for i in range(IT)]

        block_in = [sem(f"block_in{i}") for i in range(max(ADJ_SLOTS, EDGE_SLOTS))]
        edge_stored = [sem(f"edge_stored{i}") for i in range(OUT_SLOTS)]
        edge_ready = sem("edge_ready")
        next_edge_ready = sem("next_edge_ready")
        rows_in = sem("rows_in")
        above_scalar = sem("above_scalar")
        above_vector = sem("above_vector")
        pos_ready = sem("pos_ready")
        masks_ready = sem("masks_ready")
        masks_used = sem("masks_used")
        sums_done = sem("sums_done")
        pos_out, neg_out = sem("pos_out"), sem("neg_out")
        sums_used = sem("sums_used")
        x_in, y_ready, y_stored = sem("x_in"), sem("y_ready"), sem("y_stored")
        res_ready, stats_ready, moments_ready = (sem("res_ready"), sem("stats_ready"),
                                                 sem("moments_ready"))
        pool_seq, consts_ready = sem("pool_seq"), sem("consts_ready")
        passed = {e: sem(f"passed_{e}") for e in ("act", "dve", "pe", "pool", "sp")}

        pv = parts[:, 0:BRANCHES * tiles * H * HC].rearrange("p (b g c) -> p b g c", b=BRANCHES, c=HC)
        block = ctx.enter_context(nc.Block())

        @block.sync
        def _(sp):
            n_slots = ADJ_SLOTS if first else EDGE_SLOTS
            slot_sb = adj_sb if first else edge
            src = adj if first else edge_bytes

            def load(slab, c):
                sp.dma_start(slot_sb[c % n_slots][:, :],
                             src[bass.ds(slab * nb + c, 1), :, :]
                             .rearrange("a p n -> (a p) n")).then_inc(block_in[c % n_slots], 16)

            def load_rows(slab):
                for h in range(H):
                    sp.dma_start(s_rows[:, bass.ds((slab % 2) * (H * SLAB) + h * SLAB, SLAB)],
                                 score_row_dram[h:h + 1, bass.ds(slab * SLAB, SLAB)]
                                 .partition_broadcast(P).rearrange("p a n -> p (a n)")
                                 ).then_inc(rows_in, 16)

            def slab_loads(slab, last):
                for c in range(nb):
                    if first:
                        stand(sp.wait_ge(next_edge_ready, slab * nb + (c + 1)), passed["sp"])
                        sp.dma_start(edge_bytes[bass.ds(slab * nb + c, 1), :, :]
                                     .rearrange("a p n -> (a p) n"), next_edge[c % OUT_SLOTS][:, :]).then_inc(edge_stored[c % OUT_SLOTS], 16)
                    else:
                        stand(sp.wait_ge(masks_ready, slab * nb + (c + 1)), passed["sp"])
                    if not last or c + n_slots < nb:
                        load(slab, c + n_slots)
                    if c == nb // 2 and not last:
                        stand(sp.wait_ge(masks_ready, slab * nb + 1), passed["sp"])
                        load_rows(slab + 1)

            load_rows(0)
            for c in range(n_slots):
                load(0, c)
            with sp.Fori(0, slabs - 1) as slab:
                slab_loads(slab, False)
            slab_loads(slabs - 1, True)
            if first:
                for i in range(OUT_SLOTS):
                    sp.wait_ge(edge_stored[i], 16 * (slabs * nb // OUT_SLOTS + 1))

        def above_row(slab, h):
            return s_rows[:, bass.ds((slab % 2) * (H * SLAB) + h * SLAB, SLAB)]

        def scalar_does(h, t):
            return (h * JB + t) % (H * JB) in act_heads

        def row_tile_done(eng, slab, i):
            if i < IT - 1:
                return eng.wait_ge(sums_done, slab * (IT - 1) + (i + 1))
            return eng.wait_ge(masks_used, slab * nb + (nb + MASK_SLOTS))

        @block.scalar
        def _(act):
            def above_block(slab, c):
                m = c % MASK_SLOTS
                if c % nb == 0:
                    stand(act.wait_ge(rows_in, slab * (16 * H) + (c // nb + 1) * (16 * H)), passed["act"])
                stand(act.wait_ge(pos_ready, slab * nb + (c + 1)), passed["act"])
                for h in range(H):
                    for t in range(JB):
                        if scalar_does(h, t):
                            last = nc.scalar.activation(
                                above[m][:, h, t * SLAB:(t + 1) * SLAB],
                                above_row(slab + c // nb, h), ACT.Sign,
                                bias=cols["t_neg"][:, (c % nb) * JB + t, h:h + 1], scale=-1.0)
                last.then_inc(above_scalar, 1)

            def copy_out(slab):
                stand(act.wait_ge(sums_used, slab + 1), passed["act"])
                for i in range(IT):
                    stand(row_tile_done(act, slab, i), passed["act"])
                    nc.scalar.activation(sums[:, i, 1].rearrange("p h k w -> p (h k w)"),
                                         sum_ps[i][1][:, 0:H * HC], ACT.Copy).then_inc(neg_out, 1)

            for c in range(ahead):
                above_block(0, c)

            def slab_work(slab, last):
                for c in range(ahead, nb + (0 if last else 1)):
                    above_block(slab, c)
                copy_out(slab)
                if not last:
                    for c in range(nb + 1, nb + ahead):
                        above_block(slab, c)

            with act.Fori(0, slabs - 1) as slab:
                slab_work(slab, False)
            slab_work(slabs - 1, True)

        @block.vector
        def _(dve):
            dve.sem_inc(pos_ready, MASK_SLOTS)
            if first:
                for i in range(OUT_SLOTS):
                    dve.sem_inc(edge_stored[i], 16)

            def masks(slab, c):
                m, at = c % MASK_SLOTS, slab * nb
                if first:
                    slot, out = c % ADJ_SLOTS, c % OUT_SLOTS
                    dve.wait_ge(block_in[slot], slab * (16 * nb // ADJ_SLOTS)
                                + 16 * (c // ADJ_SLOTS + 1))
                    nc.vector.tensor_scalar(edge[m][:, :], adj_sb[slot][:, :], 0.0, ON, ALU.is_gt,
                                            ALU.mult).then_inc(edge_ready, 1)
                    dve.wait_ge(edge_stored[out], slab * (16 * nb // OUT_SLOTS)
                                + 16 * (c // OUT_SLOTS + 1))
                    nc.vector.tensor_scalar(next_edge[out][:, :], adj_sb[slot][:, :], 0.0, ON,
                                            ALU.not_equal, ALU.mult).then_inc(next_edge_ready, 1)
                    dve.wait_ge(edge_ready, at + (c + 1))
                    edges = edge[m]
                else:
                    slot = c % EDGE_SLOTS
                    edges = edge[slot]
                    if c % nb == 0:
                        dve.wait_ge(rows_in, slab * (16 * H) + (c // nb + 1) * (16 * H))
                    for h in range(H):
                        for t in range(JB):
                            if not scalar_does(h, t):
                                last = nc.vector.tensor_scalar(
                                    above[m][:, h, t * SLAB:(t + 1) * SLAB],
                                    above_row(slab + c // nb, h),
                                    cols["t_neg"][:, (c % nb) * JB + t, h:h + 1], ON,
                                    ALU.is_gt, ALU.mult)
                    last.then_inc(above_vector, 1)
                    dve.wait_ge(above_vector, at + (c + 1))
                    dve.wait_ge(block_in[slot], slab * (16 * nb // EDGE_SLOTS)
                                + 16 * (c // EDGE_SLOTS + 1))
                dve.wait_ge(above_scalar, at + (c + 1))
                dve.wait_ge(masks_used, at + (c + 1))
                ew = edges[:, :].bitcast(I32).unsqueeze(1).broadcast_to([P, H, words])
                aw, pw, nw = (x[m][:, :, :].rearrange("p h w -> p (h w)").bitcast(I32)
                              .rearrange("p (h w) -> p h w", h=H) for x in (above, pos, neg))
                nc.vector.tensor_tensor(pw, aw, ew, ALU.bitwise_and).then_inc(pos_ready, 1)
                dve.wait_ge(pos_ready, at + (c + 1 + MASK_SLOTS))
                nc.vector.tensor_tensor(nw, pw, ew, ALU.bitwise_xor).then_inc(masks_ready, 1)

            def copy_out(slab):
                dve.wait_ge(sums_used, slab + 1)
                for i in range(IT):
                    row_tile_done(dve, slab, i)
                    nc.vector.tensor_copy(sums[:, i, 0].rearrange("p h k w -> p (h k w)"),
                                          sum_ps[i][0][:, 0:H * HC]).then_inc(pos_out, 1)

            def row_moments(slab):
                dve.wait_ge(res_ready, slab + 1)
                for i in range(IT):
                    last = nc.vector.bn_stats(stats[:, i, :], y_sb[:, i, :])
                last.then_inc(stats_ready, 1)
                stand(dve.wait_ge(stats_ready, slab + 1), passed["dve"])
                for i in range(IT):
                    last = nc.vector.bn_aggr(moments[:, i, :], stats[:, i, :])
                last.then_inc(moments_ready, 1)

            for c in range(ahead):
                masks(0, c)

            def slab_work(slab, last):
                for c in range(ahead, nb + (0 if last else 1)):
                    masks(slab, c)
                copy_out(slab)
                if not last:
                    for c in range(nb + 1, nb + ahead):
                        masks(slab, c)
                row_moments(slab)

            with dve.Fori(0, slabs - 1) as slab:
                slab_work(slab, False)
            slab_work(slabs - 1, True)

        @block.tensor
        def _(pe):
            pe.sem_inc(masks_used, MASK_SLOTS)
            with pe.Fori(0, slabs) as slab:
                for c in range(nb):
                    m = c % MASK_SLOTS
                    stand(pe.wait_ge(masks_ready, slab * nb + (c + 1)), passed["pe"])
                    for i in range(IT):
                        if c == 0:
                            stand(pe.wait_ge(pos_out, slab * IT + (i + 1)), passed["pe"])
                            stand(pe.wait_ge(neg_out, slab * IT + (i + 1)), passed["pe"])
                        for t in range(JB):
                            j = c * JB + t
                            for h in range(H):
                                for b, mask in ((0, pos), (1, neg)):
                                    at = t * SLAB + i * P
                                    last = nc.tensor.matmul(
                                        sum_ps[i][b][:, h * HC:(h + 1) * HC],
                                        mask[m][:, h, at:at + P].bitcast(FP8),
                                        pv[:, b, j * H + h, :],
                                        start=(j == 0 and h == 0), stop=(j == tiles - 1),
                                        skip_group_check=H > 1)
                        if i == IT - 1:
                            last.then_inc(masks_used, 1)
                        elif c == nb - 1:
                            last.then_inc(sums_done, 1)

        @block.gpsimd
        def _(pool):
            pool.sem_inc(pos_out, IT)
            pool.sem_inc(neg_out, IT)
            pool.sem_inc(sums_used, 1)
            pool.dma_start(x_sb[:, :, :], x_dram[0:SLAB, :].rearrange("(t p) d -> p t d", p=P)
                           ).then_inc(x_in, 16)
            nc.gpsimd.memset(power[:, :], -1.0).then_inc(consts_ready, 1)
            nc.gpsimd.memset(half[:, :], -0.5).then_inc(consts_ready, 1)
            pool.wait_ge(consts_ready, 2)
            def finish_slab(slab, last_slab):
                per_slab = 9
                steps = [0]

                def link(instruction):
                    steps[0] += 1
                    instruction.then_inc(pool_seq, 1)
                    stand(pool.wait_ge(pool_seq, slab * per_slab + steps[0]), passed["pool"])

                factor = [cols[k][:, :, :].rearrange("p t h -> p (t h)")
                          [:, bass.ds(slab * G, G)].unsqueeze(2).broadcast_to([P, G, W])
                          for k in ("alpha", "beta")]
                flat = [a[:, :, :, :].rearrange("p i h w -> p (i h) w") for a in acc]
                stand(pool.wait_ge(pos_out, slab * IT + 2 * IT), passed["pool"])
                stand(pool.wait_ge(neg_out, slab * IT + 2 * IT), passed["pool"])
                for b in range(BRANCHES):
                    op = nc.gpsimd.tensor_tensor(acc[b][:, :, :, :], sums[:, :, b, :, 1, :],
                                                 sums[:, :, b, :, 2, :], ALU.add)
                link(op)
                for b in range(BRANCHES):
                    op = nc.gpsimd.tensor_tensor(acc[b][:, :, :, :], acc[b][:, :, :, :],
                                                 sums[:, :, b, :, 0, :], ALU.add)
                link(op)
                pool.sem_inc(sums_used, 1)
                for b in range(BRANCHES):
                    op = nc.gpsimd.tensor_tensor(flat[b], flat[b], factor[b], ALU.mult)
                link(op)
                link(nc.gpsimd.tensor_tensor(flat[0], flat[0], flat[1], ALU.add))
                link(nc.gpsimd.tensor_tensor(inv[:, :], flat[0][:, :, W - 1], power[:, :], ALU.pow))
                stand(pool.wait_ge(x_in, slab * 16 + 16), passed["pool"])
                y = y_sb[:, :, :].rearrange("p i (h w) -> p (i h) w", h=H)
                link(nc.gpsimd.tensor_tensor(y, flat[0][:, :, 0:W - 1],
                                             inv[:, :].unsqueeze(2).broadcast_to([P, G, W - 1]),
                                             ALU.mult))
                nc.gpsimd.tensor_tensor(y_sb[:, :, :], y_sb[:, :, :], x_sb[:, :, :],
                                        ALU.add).then_inc(res_ready, 1)
                stand(pool.wait_ge(res_ready, slab + 1), passed["pool"])
                if not last_slab:
                    pool.dma_start(x_sb[:, :, :],
                                   x_dram[bass.ds((slab + 1) * SLAB, SLAB), :]
                                   .rearrange("(t p) d -> p t d", p=P)).then_inc(x_in, 16)
                stand(pool.wait_ge(moments_ready, slab + 1), passed["pool"])
                link(nc.gpsimd.tensor_scalar(rstd[:, :], moments[:, :, 1], EPS, None, ALU.add))
                link(nc.gpsimd.tensor_tensor(rstd[:, :], rstd[:, :], half[:, :], ALU.pow))
                link(nc.gpsimd.tensor_tensor(y_sb[:, :, :], y_sb[:, :, :],
                                             moments[:, :, 0:1].broadcast_to([P, IT, P]),
                                             ALU.subtract))
                nc.gpsimd.tensor_tensor(y_sb[:, :, :], y_sb[:, :, :],
                                        rstd[:, :].unsqueeze(2).broadcast_to([P, IT, P]),
                                        ALU.mult).then_inc(y_ready, 1)
                stand(pool.wait_ge(y_ready, slab + 1), passed["pool"])
                pool.dma_start(out_dram[bass.ds(slab * SLAB, SLAB), :]
                               .rearrange("(t p) d -> p t d", p=P), y_sb[:, :, :]
                               ).then_inc(y_stored, 16)
                stand(pool.wait_ge(y_stored, slab * 16 + 16), passed["pool"])

            with pool.Fori(0, slabs - 1) as slab:
                finish_slab(slab, False)
            finish_slab(slabs - 1, True)


def build(nc, adj, x, x_t, proj0, proj0_t, att0, proj1, proj1_t, att1_src, att1_dst, out):
    n = x.shape[0]
    tiles = n // P
    layers = [Layer(0, 1), Layer(1, 4)]
    blocks = (n // SLAB) * (tiles // JB)
    edge_bytes = nc.dram_tensor("edge_bytes", [blocks, P, JB * SLAB], I8, kind="Internal").ap()
    x1 = nc.dram_tensor("x1", [n, P], FP32, kind="Internal").ap()
    rows = [nc.dram_tensor(f"score_rows{L.index}", [L.heads, n], FP32, kind="Internal").ap()
            for L in layers]
    with ExitStack() as keep:
        width = max(BRANCHES * tiles * L.heads * L.head_cols for L in layers)
        parts = keep.enter_context(nc.sbuf_tensor("parts", [P, width], BF16))
        cols = [{k: keep.enter_context(nc.sbuf_tensor(f"{k}{L.index}", [P, tiles, L.heads], FP32))
                 for k in ("t_neg", "alpha", "beta")} for L in layers]
        project(nc, keep, layers[0], None, x_t, proj0, proj0_t, [att0], rows[0], parts, cols[0], n)
        attend(nc, keep, layers[0], adj, edge_bytes, x, x1, rows[0], parts, cols[0], n,
               act_heads=range(4))
        project(nc, keep, layers[1], x1, None, proj1, proj1_t,
                [[a[h:h + 1, :].rearrange("a d -> d a") for h in range(4)]
                 for a in (att1_src, att1_dst)], rows[1], parts, cols[1], n)
        attend(nc, keep, layers[1], None, edge_bytes, x1, out, rows[1], parts, cols[1], n,
               act_heads=SCALAR_SHARE)


def kernel(x, adj, L0_gnn_Ws, L0_gnn_a, L1_gnn_W, L1_gnn_attn_src, L1_gnn_attn_dst):
    import numpy as np
    import concourse.bacc as bacc
    from concourse.bass_utils import run_bass_kernel_spmd

    x, adj = np.asarray(x), np.asarray(adj)
    n = x.shape[0]
    tiles, slabs = n // P, n // SLAB
    blocks = adj.reshape(slabs, SLAB, tiles // JB, JB, P).transpose(0, 2, 4, 3, 1)
    Ws, W1 = np.asarray(L0_gnn_Ws), np.asarray(L1_gnn_W)
    arrays = {
        "adj": blocks.reshape(slabs * (tiles // JB), P, JB * SLAB),
        "x": x,
        "x_t": x.T,
        "proj0": Ws,
        "proj0_t": Ws.T,
        "att0": np.asarray(L0_gnn_a).reshape(2, P).T,
        "proj1": W1.T,
        "proj1_t": W1,
        "att1_src": np.asarray(L1_gnn_attn_src)[0],
        "att1_dst": np.asarray(L1_gnn_attn_dst)[0],
    }
    arrays = {k: np.ascontiguousarray(v) for k, v in arrays.items()}
    nc = bacc.Bacc("TRN2", target_bir_lowering=False, num_devices=1)
    args = [nc.dram_tensor(k, v.shape, mybir.dt.from_np(v.dtype), kind="ExternalInput").ap()
            for k, v in arrays.items()]
    out = nc.dram_tensor("out", [n, P], FP32, kind="ExternalOutput").ap()
    build(nc, *args, out)
    return run_bass_kernel_spmd(nc, [arrays], core_ids=[0]).results[0]["out"]
```

```python
from contextlib import ExitStack

import concourse.bass as bass
from concourse import mybir

FP32, BF16, FP16 = mybir.dt.float32, mybir.dt.bfloat16, mybir.dt.float16
I8, I32, FP8 = mybir.dt.int8, mybir.dt.int32, mybir.dt.float8e4
ALU = mybir.AluOpType
ACT = mybir.ActivationFunctionType
AX = mybir.AxisListType

P = 128
JB = 4
STRIP = 512
BANKS = 8
POS_PARTS = 3
NEG_PARTS = 2
NEG_TOP = 2.0 ** 14
ON = 64.0
SLOPE = 0.2
EPS = 1e-5
ADJ_SLOTS = 4
OUT_SLOTS = 4
EDGE_SLOTS = 4
MASK_SLOTS = 2
FEAT_SLOTS = 4


class Layer:

    def __init__(self, index, heads, sweeps, strips, whole, scalar_share):
        self.index, self.heads = index, heads
        self.sweeps = sweeps
        self.sweep_heads = heads // sweeps
        self.strips = strips
        self.slab = strips * STRIP
        self.whole = whole
        self.scalar_share = scalar_share
        self.width = P // heads + 1
        self.pos_cols = POS_PARTS * self.width
        self.neg_cols = NEG_PARTS * self.width
        self.pos_step = self.pos_cols + 1
        self.name = f"l{index}_"

    def allocate(self, nc, ctx, tiles):
        sb = lambda s, shape, dt: ctx.enter_context(nc.sbuf_tensor(self.name + s, shape, dt))
        S, H, W = self.sweeps, self.sweep_heads, self.width
        self.v_pos = sb("v_pos", [P, S, tiles * H, self.pos_step], BF16)
        self.v_neg = sb("v_neg", [P, S, tiles * H, NEG_PARTS, W], FP16)
        self.t_neg = sb("t_neg", [P, S, tiles, H], FP32)
        self.alpha = sb("alpha", [P, S, tiles, H], FP32)
        self.beta = sb("beta", [P, S, tiles, H], FP32)
        self.wgt = sb("wgt", [P, 2, S, tiles, H], FP32)
        self.all_sum = sb("all_sum", [P, W], FP32) if self.index == 0 else None

    def group(self, g):
        return slice(g * JB * self.sweep_heads, (g + 1) * JB * self.sweep_heads)

    def kept(self, s, g):
        return self.v_pos[:, s, self.group(g), self.width + 3:self.pos_step].bitcast(FP32)

    def pos_part(self, s, g, k):
        return self.v_pos[:, s, self.group(g), k * self.width:(k + 1) * self.width]


def stand(wait, passed):
    wait.then_inc(passed, 1)


def chain(eng, sem):
    count = [0]

    def link(instruction):
        count[0] += 1
        instruction.then_inc(sem, 1)
        eng.wait_ge(sem, count[0])

    return link


def project(nc, keep, L, x_dram, feat_t_dram, proj, proj_t, att, score_row_dram, n):
    H, W = L.heads, L.width
    tiles = n // P
    groups = tiles // JB
    gw = JB * P
    name = L.name
    S, SH = L.sweeps, L.sweep_heads
    pairs = H * tiles
    rb = min(P, pairs)
    row_blocks = pairs // rb
    transposed = x_dram is None
    with ExitStack() as ctx:
        sb = lambda s, shape, dt: ctx.enter_context(nc.sbuf_tensor(name + s, shape, dt))
        pb = lambda s, shape, dt: ctx.enter_context(nc.psum_tensor(name + s, shape, dt))
        sem = lambda s: keep.enter_context(nc.semaphore(name + s))

        feat_t = sb("feat_t", [P, n], FP32)
        feat = None if transposed else sb("feat", [P, FEAT_SLOTS, JB, P], FP32)
        ident = sb("ident", [P, P], FP32)
        proj_sb = sb("proj_sb", [P, P], FP32)
        proj_t_sb = sb("proj_t_sb", [P, P], FP32)
        att_sb = sb("att_sb", [P, 2 * H], FP32)
        watt = sb("watt", [P, 2 * H], FP32)
        scores = sb("scores", [P, 2 * H, tiles], FP32)
        row_sb = sb("row_sb", [P, row_blocks, P], FP32)
        val_max = sb("val_max", [P, S * groups], FP32)
        pmax = sb("pmax", [P, H + 1], FP32)
        gmax = sb("gmax", [P, H + 1], FP32)
        up = sb("up", [P, 1], FP32)
        down = sb("down", [P, 1], FP32)
        z_t = sb("z_t", [P, S, tiles, SH], FP32)
        z_s = sb("z_s", [P, S, tiles, SH], FP32)
        z_alpha = sb("z_alpha", [P, S, tiles, SH], FP32)
        z_beta = sb("z_beta", [P, S, tiles, SH], FP32)
        part_sum = sb("part_sum", [P, groups], FP32)
        feat_sum = sb("feat_sum", [P, 1], FP32)
        feat_sums = sb("feat_sums", [P, P], FP32)

        tr_ps = [pb(f"tr_ps{i}", [P, gw], FP32) for i in range(2)]
        val_ps = [pb(f"val_ps{i}", [P, gw], FP32) for i in range(2)]
        row_ps = pb("row_ps", [P, row_blocks, P], FP32)
        score_ps = pb("score_ps", [P, 512], FP32)
        watt_ps = pb("watt_ps", [P, 2 * H], FP32)
        sum_ps = pb("sum_ps", [P, P], FP32)

        weights_in, att_ready = sem("weights_in"), sem("att_ready")
        feat_in = [sem(f"feat_in{i}") for i in range(groups // 2 if transposed else FEAT_SLOTS)]
        ident_zero, ident_ready = sem("ident_zero"), sem("ident_ready")
        watt_done, watt_ready = sem("watt_done"), sem("watt_ready")
        tr_done, feat_t_ready = sem("tr_done"), sem("feat_t_ready")
        val_done, val_kept, val_max_ready = sem("val_done"), sem("val_kept"), sem("val_max_ready")
        scores_done, scores_ready = sem("scores_done"), sem("scores_ready")
        rows_done, rows_ready, rows_stored = sem("rows_done"), sem("rows_ready"), sem("rows_stored")
        pmax_ready, gmax_ready = sem("pmax_ready"), sem("gmax_ready")
        z_ready, expo_done, dve_seq = sem("z_ready"), sem("expo_done"), sem("dve_seq")
        feat_sums_ready, all_sum_done = sem("feat_sums_ready"), sem("all_sum_done")

        n_weights = 2 if H == 1 else 2 + 2 * H
        block = ctx.enter_context(nc.Block())

        @block.sync
        def _(sp):
            def load_feat(g):
                sp.dma_start(feat[:, g % FEAT_SLOTS],
                             x_dram[g * gw:(g + 1) * gw, :].rearrange("(t p) d -> p t d", p=P)
                             ).then_inc(feat_in[g % FEAT_SLOTS], 16)

            sp.dma_start(proj_sb[:, :], proj).then_inc(weights_in, 16)
            sp.dma_start(proj_t_sb[:, :], proj_t).then_inc(weights_in, 16)
            if transposed:
                for g in range(0, groups, 2):
                    sp.dma_start(feat_t[:, g * gw:(g + 2) * gw],
                                 feat_t_dram[:, g * gw:(g + 2) * gw]).then_inc(feat_in[g // 2], 16)
            else:
                for g in range(FEAT_SLOTS):
                    load_feat(g)
            if H == 1:
                sp.dma_start(att_sb[:, :], att[0]).then_inc(att_ready, 16)
            else:
                sp.wait_ge(att_ready, 1)
                for k in range(2):
                    for h in range(H):
                        d = P // H
                        sp.dma_start(att_sb[h * d:(h + 1) * d, k * H + h:k * H + h + 1],
                                     att[k][h]).then_inc(weights_in, 16)
            if not transposed:
                for g in range(FEAT_SLOTS, groups):
                    sp.wait_ge(tr_done, g - FEAT_SLOTS + 1)
                    load_feat(g)
            row_pairs = score_row_dram.rearrange("h (t p) -> (h t) p", p=P)
            for r in range(row_blocks):
                sp.wait_ge(rows_ready, 1)
                sp.dma_start(row_pairs[r * rb:(r + 1) * rb, :],
                             row_sb[0:rb, r, :]).then_inc(rows_stored, 16)
            sp.wait_ge(rows_stored, 16 * row_blocks)

        @block.gpsimd
        def _(pool):
            nc.gpsimd.memset(ident[:, :], 0.0).then_inc(ident_zero, 1)
            pool.wait_ge(ident_zero, 1)
            nc.gpsimd.affine_select(out=ident[:, :], in_=ident[:, :], compare_op=ALU.not_equal,
                                    fill=1.0, base=0, pattern=[[-1, P]],
                                    channel_multiplier=1).then_inc(ident_ready, 1)
            pool.wait_ge(pmax_ready, 2)
            nc.gpsimd.partition_all_reduce(gmax[:, :], pmax[:, :], P,
                                           bass.bass_isa.ReduceOp.max).then_inc(gmax_ready, 1)

        @block.tensor
        def _(pe):
            def transpose(g):
                pe.wait_ge(feat_in[g % FEAT_SLOTS], 16 * (g // FEAT_SLOTS + 1))
                if g >= 2:
                    pe.wait_ge(feat_t_ready, g - 1)
                for t in range(JB):
                    last = nc.tensor.transpose(tr_ps[g % 2][:, t * P:(t + 1) * P],
                                               feat[:, g % FEAT_SLOTS, t, :], ident[:, :])
                last.then_inc(tr_done, 1)

            pe.wait_ge(weights_in, 16 * n_weights)
            if H == 1:
                pe.wait_ge(att_ready, 16)
            nc.tensor.matmul(watt_ps[:, :], proj_t_sb[:, :], att_sb[:, :], start=True,
                             stop=True).then_inc(watt_done, 1)
            pe.wait_ge(ident_ready, 1)
            if not transposed:
                transpose(0)
            pe.wait_ge(watt_ready, 1)
            for g in range(groups):
                if transposed:
                    pe.wait_ge(feat_in[g // 2], 16)
                else:
                    if g + 1 < groups:
                        transpose(g + 1)
                    pe.wait_ge(feat_t_ready, g + 1)
                if g >= 2:
                    pe.wait_ge(val_kept, g - 1)
                for t in range(JB):
                    last = nc.tensor.matmul(val_ps[g % 2][:, t * P:(t + 1) * P],
                                            feat_t[:, (g * JB + t) * P:(g * JB + t + 1) * P],
                                            proj_sb[:, :], start=True, stop=True)
                last.then_inc(val_done, 1)
                for t in range(g * JB, (g + 1) * JB):
                    last = nc.tensor.matmul(score_ps[:, t * 2 * H:(t + 1) * 2 * H],
                                            feat_t[:, t * P:(t + 1) * P], watt[:, :],
                                            start=True, stop=True)
            last.then_inc(scores_done, 1)
            pe.wait_ge(scores_ready, 1)
            s_flat = scores[:, 0:H, :].rearrange("p h t -> p (h t)")
            for r in range(row_blocks):
                last = nc.tensor.transpose(row_ps[0:rb, r, :], s_flat[:, r * rb:(r + 1) * rb],
                                           ident[:, :])
            last.then_inc(rows_done, 1)
            if L.all_sum is not None:
                pe.wait_ge(feat_sums_ready, 1)
                nc.tensor.matmul(sum_ps[:, :], feat_sums[:, :], proj_sb[:, :], start=True,
                                 stop=True).then_inc(all_sum_done, 1)

        @block.scalar
        def _(act):
            for g in range(groups):
                act.wait_ge(val_done, g + 1)
                by_sweep = val_ps[g % 2][:, :].rearrange("p (t s h w) -> p s t h w", t=JB, s=S, h=SH)
                for s in range(S):
                    last = nc.scalar.activation(
                        L.kept(s, g).rearrange("p (t h) w -> p t h w", h=SH), by_sweep[:, s],
                        ACT.Copy)
                last.then_inc(val_kept, 1)
            act.wait_ge(rows_done, 1)
            nc.scalar.activation(row_sb[0:rb, :, :], row_ps[0:rb, :, :],
                                 ACT.Copy).then_inc(rows_ready, 1)
            act.wait_ge(z_ready, 1)
            nc.scalar.activation(L.wgt[:, 0], z_t[:, :, :, :], ACT.Exp)
            nc.scalar.activation(z_t[:, :, :, :], z_t[:, :, :, :], ACT.Exp,
                                 scale=SLOPE).then_inc(expo_done, 1)
            act.wait_ge(z_ready, 2)
            nc.scalar.activation(L.alpha[:, :, :, :], z_alpha[:, :, :, :], ACT.Exp)
            nc.scalar.activation(z_beta[:, :, :, :], z_beta[:, :, :, :], ACT.Exp).then_inc(expo_done, 1)

        @block.vector
        def _(dve):
            link = chain(dve, dve_seq)
            if H > 1:
                nc.vector.memset(att_sb[:, :], 0.0).then_inc(att_ready, 1)
            dve.wait_ge(watt_done, 1)
            nc.vector.tensor_copy(watt[:, :], watt_ps[:, :]).then_inc(watt_ready, 1)

            def copy_feat(g):
                dve.wait_ge(tr_done, g + 1)
                nc.vector.tensor_copy(feat_t[:, g * gw:(g + 1) * gw],
                                      tr_ps[g % 2][:, :]).then_inc(feat_t_ready, 1)

            if not transposed:
                copy_feat(0)
            for g in range(groups):
                if not transposed and g + 1 < groups:
                    copy_feat(g + 1)
                if L.all_sum is not None:
                    dve.wait_ge(feat_in[g // 2], 16)
                    nc.vector.reduce_sum(part_sum[:, g:g + 1], feat_t[:, g * gw:(g + 1) * gw],
                                         axis=AX.X)
                dve.wait_ge(val_kept, g + 1)
                for s in range(S):
                    nc.vector.tensor_reduce(val_max[:, s * groups + g:s * groups + g + 1],
                                            L.kept(s, g), AX.XY, ALU.max,
                                            apply_absolute_value=True).then_inc(val_max_ready, 1)
            dve.wait_ge(scores_done, 1)
            nc.vector.tensor_copy(scores[:, :, :].rearrange("p c t -> p t c"),
                                  score_ps[:, 0:tiles * 2 * H].rearrange("p (t c) -> p t c", c=2 * H)
                                  ).then_inc(scores_ready, 1)
            dve.wait_ge(scores_ready, 1)
            s_cols = scores[:, 0:H, :].rearrange("p (s h) t -> p s t h", s=S)
            t_cols = scores[:, H:2 * H, :].rearrange("p (s h) t -> p s t h", s=S)
            nc.vector.tensor_reduce(pmax[:, 0:H], scores[:, H:2 * H, :], AX.X,
                                    ALU.max).then_inc(pmax_ready, 1)
            dve.wait_ge(val_max_ready, S * groups)
            link(nc.vector.tensor_reduce(up[:, :], val_max[:, :], AX.X, ALU.max))
            nc.vector.tensor_scalar(pmax[:, H:H + 1], up[:, :], 1.0, None,
                                    ALU.max).then_inc(pmax_ready, 1)
            link(nc.vector.tensor_scalar(L.t_neg[:, :, :, :], t_cols, -1.0, None, ALU.mult))
            if L.all_sum is not None:
                link(nc.vector.reduce_sum(feat_sum[:, :], part_sum[:, :], axis=AX.X))
                nc.vector.tensor_copy(feat_sums[:, :],
                                      feat_sum[:, :].broadcast_to([P, P])).then_inc(feat_sums_ready, 1)
            top = (gmax[:, 0:H].rearrange("p (s h) -> p s h", s=S).unsqueeze(2)
                   .broadcast_to([P, S, tiles, SH]))
            dve.wait_ge(gmax_ready, 1)
            nc.vector.tensor_tensor(z_t[:, :, :, :], t_cols, top, ALU.subtract).then_inc(z_ready, 1)
            link(nc.vector.tensor_tensor(z_s[:, :, :, :], s_cols, top, ALU.add))
            nc.vector.tensor_scalar(z_alpha[:, :, :, :], z_s[:, :, :, :], 1.0 - SLOPE, 0.0, ALU.mult,
                                    ALU.min)
            nc.vector.tensor_scalar(z_beta[:, :, :, :], z_s[:, :, :, :], SLOPE - 1.0, 0.0, ALU.mult,
                                    ALU.min).then_inc(z_ready, 1)
            link(nc.vector.tensor_scalar(down[:, :], gmax[:, H:H + 1], 1.0 / NEG_TOP, None,
                                         ALU.mult))
            link(nc.vector.reciprocal(up[:, :], down[:, :]))
            dve.wait_ge(expo_done, 1)
            nc.vector.tensor_scalar(L.wgt[:, 1], z_t[:, :, :, :], up[:, :], None, ALU.mult)
            dve.wait_ge(expo_done, 2)
            nc.vector.tensor_scalar(L.beta[:, :, :, :], z_beta[:, :, :, :], down[:, :], None, ALU.mult)
            if L.all_sum is not None:
                nc.vector.memset(L.all_sum[:, W - 1:W], float(n))
                dve.wait_ge(all_sum_done, 1)
                nc.vector.tensor_copy(L.all_sum[:, 0:W - 1], sum_ps[:, :])


def attend(nc, keep, L, sweep, adj, edge_bytes, residual, out_dram, score_row_dram, passed, n):
    H, W, PC, NC, K = L.sweep_heads, L.width, L.pos_cols, L.neg_cols, L.whole
    tiles = n // P
    slabs = n // L.slab
    rows = L.slab
    IT = rows // P
    nb = tiles // JB
    ahead = max(1, nb // 2 - 1)
    store_at = nb * 3 // 4
    words = JB * rows // 4
    first = L.index == 0
    closes = sweep == L.sweeps - 1
    head0 = sweep * H
    name = f"{L.name}{sweep}_"
    G = IT * H
    cols = slice(head0 * (W - 1), (head0 + H) * (W - 1)) if closes else slice(0, H * (W - 1))
    row_width = P if closes else H * (W - 1)
    with ExitStack() as ctx:
        sb = lambda s, shape, dt: ctx.enter_context(nc.sbuf_tensor(name + s, shape, dt))
        sem = lambda s: keep.enter_context(nc.semaphore(name + s))

        s_rows = sb("s_rows", [P, 2 * H * rows], FP32)
        above = [sb(f"above{i}", [P, H, JB * rows], I8) for i in range(MASK_SLOTS)]
        pos = [sb(f"pos{i}", [P, H, JB * rows], I8) for i in range(MASK_SLOTS)]
        neg = [sb(f"neg{i}", [P, H - K, JB * rows], I8) for i in range(MASK_SLOTS)]
        if first:
            adj_sb = [sb(f"adj_sb{i}", [P, JB * rows], I32) for i in range(ADJ_SLOTS)]
            edge = [sb(f"edge{i}", [P, JB * rows], I8) for i in range(MASK_SLOTS)]
            next_edge = [sb(f"next_edge{i}", [P, JB * rows], I8) for i in range(OUT_SLOTS)]
        else:
            edge = [sb(f"edge{i}", [P, JB * rows], I8) for i in range(EDGE_SLOTS)]
        v_sub = sb("v_sub", [P, tiles, K, NEG_PARTS, W], FP16) if K else None
        full = sb("full", [P, 2, JB * H, W], FP32)
        rest = sb("rest", [P, 2, JB * H, W], FP32)
        sums = sb("sums", [P, IT, H, POS_PARTS + NEG_PARTS, W], FP32)
        acc = [sb(f"acc{b}", [P, IT, H, W], FP32) for b in range(2)]
        x_sb = sb("x_sb", [P, IT, row_width], FP32)
        y_sb = sb("y_sb", [P, IT, row_width], FP32)
        inv = sb("inv", [P, G], FP32)
        minus_one = sb("minus_one", [P, G], FP32)
        minus_half = sb("minus_half", [P, IT], FP32)
        stats = sb("stats", [P, IT, 6], FP32)
        moments = sb("moments", [P, IT, 2], FP32)
        rstd = sb("rstd", [P, IT], FP32)
        lone = sb("lone", [P, G], FP32)
        banks = [ctx.enter_context(nc.psum_tensor(f"{name}bank{i}", [P, 512], FP32))
                 for i in range(BANKS)]

        def bank_of(i, negative):
            return 2 * i + negative if IT * 2 == BANKS else i

        def column_of(h, negative):
            if IT * 2 == BANKS:
                return h * (NC if negative else PC)
            return h * (PC + NC) + (PC if negative else 0)

        def sums_of(b):
            if IT * 2 == BANKS:
                i, negative = divmod(b, 2)
                part = slice(POS_PARTS, POS_PARTS + NEG_PARTS) if negative else slice(0, POS_PARTS)
                return banks[b][:, 0:H * (NC if negative else PC)], i, sums[:, i, 0, part]
            return banks[b][:, 0:H * (PC + NC)], b, sums[:, b].rearrange("p h k w -> p (h k) w")

        block_in = [sem(f"block_in{i}") for i in range(max(ADJ_SLOTS, EDGE_SLOTS))]
        if first:
            edge_stored = [sem(f"edge_stored{i}") for i in range(OUT_SLOTS)]
            edge_ready = sem("edge_ready")
            next_edge_ready = sem("next_edge_ready")
        rows_in = sem("rows_in")
        above_scalar = sem("above_scalar")
        above_vector = sem("above_vector")
        pos_ready = sem("pos_ready")
        masks_ready = sem("masks_ready")
        masks_used = sem("masks_used")
        sums_done = sem("sums_done")
        out_vector, out_scalar = sem("out_vector"), sem("out_scalar")
        sums_used = sem("sums_used")
        x_in, y_ready, y_stored = sem("x_in"), sem("y_ready"), sem("y_stored")
        if closes:
            res_ready, stats_ready, moments_ready = (sem("res_ready"), sem("stats_ready"),
                                                     sem("moments_ready"))
        pool_seq, consts_ready = sem("pool_seq"), sem("consts_ready")
        full_ready, hi_ready, rest_ready = sem("full_ready"), sem("hi_ready"), sem("rest_ready")
        mid_ready = sem("mid_ready")
        scalar_parts = sem("scalar_parts")
        last_parts = sem("last_parts")
        if K:
            sub_ready = sem("sub_ready")

        block = ctx.enter_context(nc.Block())

        @block.sync
        def _(sp):
            n_slots = ADJ_SLOTS if first else EDGE_SLOTS
            slot_sb = adj_sb if first else edge
            src = adj if first else edge_bytes

            src_blocks = src.rearrange("(s k c) p n -> s c p k n", k=L.strips, c=nb)

            def load(slab, c):
                sp.dma_start(slot_sb[c % n_slots][:, :].rearrange("p (k n) -> p k n", k=L.strips),
                             src_blocks[bass.ds(slab + c // nb, 1), c % nb, :, :, :]
                             .rearrange("a p k n -> (a p) k n")).then_inc(block_in[c % n_slots], 16)

            def load_rows(slab):
                for h in range(H):
                    sp.dma_start(s_rows[:, bass.ds((slab % 2) * (H * rows) + h * rows, rows)],
                                 score_row_dram[head0 + h:head0 + h + 1,
                                                bass.ds(slab * rows, rows)]
                                 .partition_broadcast(P).rearrange("p a n -> p (a n)")
                                 ).then_inc(rows_in, 16)

            def row_tiles(dram, slab):
                return dram[bass.ds(slab * rows, rows), :].rearrange("(t p) d -> p t d", p=P)

            def load_residual(slab):
                for dram, at in residual:
                    sp.dma_start(x_sb[:, :, at:at + dram.shape[1]],
                                 row_tiles(dram, slab)).then_inc(x_in, 16)

            def store(slab):
                stand(sp.wait_ge(y_ready, slab + 1), passed["sp"])
                sp.dma_start(row_tiles(out_dram, slab), y_sb[:, :, :]).then_inc(y_stored, 16)

            def slab_loads(slab, opening, last):
                for c in range(nb):
                    if first:
                        stand(sp.wait_ge(next_edge_ready, slab * nb + (c + 1)), passed["sp"])
                        sp.dma_start(edge_bytes[bass.ds(slab * nb + c, 1), :, :]
                                     .rearrange("a p n -> (a p) n"), next_edge[c % OUT_SLOTS][:, :]
                                     ).then_inc(edge_stored[c % OUT_SLOTS], 16)
                    else:
                        stand(sp.wait_ge(masks_used, slab * nb + (c + 1 + MASK_SLOTS)), passed["sp"])
                    if not last or c + n_slots < nb:
                        load(slab, c + n_slots)
                    if c == nb // 2 and not last:
                        stand(sp.wait_ge(masks_ready, slab * nb + 1), passed["sp"])
                        load_rows(slab + 1)
                    if c == store_at and not opening:
                        store(slab - 1)
                        load_residual(slab)

            load_rows(0)
            for c in range(n_slots):
                load(0, c)
            load_residual(0)
            slab_loads(0, True, False)
            with sp.Fori(1, slabs - 1) as slab:
                slab_loads(slab, False, False)
            slab_loads(slabs - 1, False, True)
            store(slabs - 1)
            sp.wait_ge(y_stored, 16 * slabs)
            if first:
                for i in range(OUT_SLOTS):
                    sp.wait_ge(edge_stored[i], 16 * (slabs * nb // OUT_SLOTS + 1))

        def above_row(slab, h):
            return (s_rows[:, bass.ds((slab % 2) * (H * rows) + h * rows, rows)]
                    .rearrange("p (k r) -> p k r", r=STRIP))

        def above_part(m, h, t):
            return above[m][:, h, :].rearrange("p (k t r) -> p k t r", t=JB, r=STRIP)[:, :, t, :]

        def comparisons(c, scalar):
            share, total = L.scalar_share[c % len(L.scalar_share)], H * JB
            return [divmod(k, JB) for k in range(total)
                    if ((k + 1) * share // total > k * share // total) == scalar]

        def row_tile_done(eng, slab, i):
            if i < IT - 1:
                return eng.wait_ge(sums_done, slab * (IT - 1) + (i + 1))
            return eng.wait_ge(masks_used, slab * nb + (nb + MASK_SLOTS))

        @block.scalar
        def _(act):
            def above_block(slab, c):
                m = c % MASK_SLOTS
                if c % nb == 0:
                    stand(act.wait_ge(rows_in, slab * (16 * H) + (c // nb + 1) * (16 * H)),
                          passed["act"])
                stand(act.wait_ge(pos_ready, slab * nb + (c + 1)), passed["act"])
                for h, t in comparisons(c, True):
                    last = nc.scalar.activation(
                        above_part(m, h, t), above_row(slab + c // nb, h), ACT.Sign,
                        bias=L.t_neg[:, sweep, (c % nb) * JB + t, h:h + 1], scale=-1.0)
                last.then_inc(above_scalar, 1)

            def first_parts(g):
                act.wait_ge(full_ready, g + 1)
                ts = slice(g * JB, (g + 1) * JB)
                by_head = full[:, 1].rearrange("p (t h) w -> p t h w", h=H)
                nc.scalar.activation(L.pos_part(sweep, g, 0), full[:, 0], ACT.Copy)
                last = nc.scalar.activation(
                    L.v_neg[:, sweep, L.group(g), 0, :], full[:, 1], ACT.Copy)
                last.then_inc(hi_ready, 1)
                for h in range(K):
                    last = nc.scalar.activation(v_sub[:, ts, h, 0, :], by_head[:, :, h, :],
                                                ACT.Copy, scale=-1.0)
                if K:
                    last.then_inc(sub_ready, 1)

            def later_parts(g):
                act.wait_ge(rest_ready, g + 1)
                ts = slice(g * JB, (g + 1) * JB)
                by_head = rest[:, 1].rearrange("p (t h) w -> p t h w", h=H)
                nc.scalar.activation(L.pos_part(sweep, g, 1), rest[:, 0], ACT.Copy).then_inc(mid_ready, 1)
                for h in range(K):
                    nc.scalar.activation(v_sub[:, ts, h, 1, :], by_head[:, :, h, :],
                                         ACT.Copy, scale=-1.0)
                nc.scalar.activation(L.v_neg[:, sweep, L.group(g), 1, :], rest[:, 1], ACT.Copy).then_inc(scalar_parts, 1)

            def copy_out(slab):
                stand(act.wait_ge(sums_used, slab + 1), passed["act"])
                for b in range(1, BANKS, 2):
                    bank, i, out = sums_of(b)
                    stand(row_tile_done(act, slab, i), passed["act"])
                    nc.scalar.activation(out.rearrange("p k w -> p (k w)"), bank,
                                         ACT.Copy).then_inc(out_scalar, 1)

            above_block(0, 0)
            for g in range(nb):
                first_parts(g)
                above_block(0, g + 1)
                later_parts(g)
            copy_out(0)
            for c in range(nb + 1, nb + ahead):
                above_block(0, c)

            def slab_work(slab, last):
                for c in range(ahead, nb + (0 if last else 1)):
                    above_block(slab, c)
                copy_out(slab)
                if not last:
                    for c in range(nb + 1, nb + ahead):
                        above_block(slab, c)

            with act.Fori(1, slabs - 1) as slab:
                slab_work(slab, False)
            slab_work(slabs - 1, True)

        @block.vector
        def _(dve):
            dve.sem_inc(pos_ready, MASK_SLOTS)
            if first:
                for i in range(OUT_SLOTS):
                    dve.sem_inc(edge_stored[i], 16)

            def masks(slab, c):
                m, at = c % MASK_SLOTS, slab * nb
                if first:
                    slot, out = c % ADJ_SLOTS, c % OUT_SLOTS
                    dve.wait_ge(block_in[slot], slab * (16 * nb // ADJ_SLOTS)
                                + 16 * (c // ADJ_SLOTS + 1))
                    nc.vector.tensor_scalar(edge[m][:, :], adj_sb[slot][:, :], 0.0, ON, ALU.is_gt,
                                            ALU.mult).then_inc(edge_ready, 1)
                    dve.wait_ge(edge_stored[out], slab * (16 * nb // OUT_SLOTS)
                                + 16 * (c // OUT_SLOTS + 1))
                    nc.vector.tensor_scalar(next_edge[out][:, :], adj_sb[slot][:, :], 0.0, ON,
                                            ALU.not_equal, ALU.mult).then_inc(next_edge_ready, 1)
                    dve.wait_ge(edge_ready, at + (c + 1))
                    edges = edge[m]
                else:
                    slot = c % EDGE_SLOTS
                    edges = edge[slot]
                    if c % nb == 0:
                        dve.wait_ge(rows_in, slab * (16 * H) + (c // nb + 1) * (16 * H))
                    for h, t in comparisons(c, False):
                        last = nc.vector.tensor_scalar(
                            above_part(m, h, t), above_row(slab + c // nb, h),
                            L.t_neg[:, sweep, (c % nb) * JB + t, h:h + 1], ON, ALU.is_gt, ALU.mult)
                    last.then_inc(above_vector, 1)
                    dve.wait_ge(above_vector, at + (c + 1))
                    dve.wait_ge(block_in[slot], slab * (16 * nb // EDGE_SLOTS)
                                + 16 * (c // EDGE_SLOTS + 1))
                dve.wait_ge(above_scalar, at + (c + 1))
                dve.wait_ge(masks_used, at + (c + 1))
                as_words = lambda x: (x[:, :, :].rearrange("p h w -> p (h w)").bitcast(I32)
                                      .rearrange("p (h w) -> p h w", w=words))
                edge_words = edges[:, :].bitcast(I32).unsqueeze(1)
                pos_words = as_words(pos[m])
                nc.vector.tensor_tensor(pos_words, as_words(above[m]),
                                        edge_words.broadcast_to([P, H, words]),
                                        ALU.bitwise_and).then_inc(pos_ready, 1)
                dve.wait_ge(pos_ready, at + (c + 1 + MASK_SLOTS))
                nc.vector.tensor_tensor(as_words(neg[m]), pos_words[:, K:H, :],
                                        edge_words.broadcast_to([P, H - K, words]),
                                        ALU.bitwise_xor).then_inc(masks_ready, 1)

            def weigh(g):
                if g:
                    dve.wait_ge(rest_ready, g)
                    dve.wait_ge(hi_ready, g)
                    if K:
                        dve.wait_ge(sub_ready, g)
                for b in range(2):
                    w = L.wgt[:, b, sweep, g * JB:(g + 1) * JB, :].rearrange("p t h -> p (t h)").unsqueeze(2)
                    nc.vector.tensor_tensor(full[:, b, :, 0:W - 1], L.kept(sweep, g),
                                            w.broadcast_to([P, JB * H, W - 1]), ALU.mult)
                    last = nc.vector.tensor_copy(full[:, b, :, W - 1:W], w)
                last.then_inc(full_ready, 1)

            def leave(g):
                dve.wait_ge(hi_ready, g + 1)
                if g:
                    dve.wait_ge(scalar_parts, g)
                    dve.wait_ge(last_parts, g)
                nc.vector.tensor_tensor(rest[:, 0], full[:, 0], L.pos_part(sweep, g, 0), ALU.subtract)
                nc.vector.tensor_tensor(
                    rest[:, 1], full[:, 1],
                    L.v_neg[:, sweep, L.group(g), 0, :],
                    ALU.subtract).then_inc(rest_ready, 1)

            def copy_out(slab):
                dve.wait_ge(sums_used, slab + 1)
                for b in range(0, BANKS, 2):
                    bank, i, out = sums_of(b)
                    row_tile_done(dve, slab, i)
                    nc.vector.tensor_copy(out.rearrange("p k w -> p (k w)"),
                                          bank).then_inc(out_vector, 1)

            def row_moments(slab):
                if not closes:
                    return
                dve.wait_ge(res_ready, slab + 1)
                for i in range(IT):
                    last = nc.vector.bn_stats(stats[:, i, :], x_sb[:, i, :])
                last.then_inc(stats_ready, 1)
                stand(dve.wait_ge(stats_ready, slab + 1), passed["dve"])
                for i in range(IT):
                    last = nc.vector.bn_aggr(moments[:, i, :], stats[:, i, :])
                last.then_inc(moments_ready, 1)

            weigh(0)
            for g in range(nb):
                masks(0, g)
                leave(g)
                if g + 1 < nb:
                    weigh(g + 1)
            masks(0, nb)
            copy_out(0)
            for c in range(nb + 1, nb + ahead):
                masks(0, c)
            row_moments(0)

            def slab_work(slab, last):
                for c in range(ahead, nb + (0 if last else 1)):
                    masks(slab, c)
                copy_out(slab)
                if not last:
                    for c in range(nb + 1, nb + ahead):
                        masks(slab, c)
                row_moments(slab)

            with dve.Fori(1, slabs - 1) as slab:
                slab_work(slab, False)
            slab_work(slabs - 1, True)

        @block.tensor
        def _(pe):
            pe.sem_inc(masks_used, MASK_SLOTS)
            with pe.Fori(0, slabs) as slab:
                for c in range(nb):
                    m = c % MASK_SLOTS
                    stand(pe.wait_ge(masks_ready, slab * nb + (c + 1)), passed["pe"])
                    pe.wait_ge(scalar_parts, c + 1)
                    pe.wait_ge(last_parts, c + 1)
                    for i in range(IT):
                        if c == 0:
                            for b in sorted({bank_of(i, 0), bank_of(i, 1)}):
                                out = out_scalar if b % 2 else out_vector
                                stand(pe.wait_ge(out, slab * (BANKS // 2) + (b // 2 + 1)),
                                      passed["pe"])
                        pos_bank, neg_bank = banks[bank_of(i, 0)], banks[bank_of(i, 1)]
                        for t in range(JB):
                            j = c * JB + t
                            at = (i // (STRIP // P) * JB + t) * STRIP + i % (STRIP // P) * P
                            begin, end = j == 0, j == tiles - 1
                            for h in range(H):
                                lo, pair = column_of(h, 1), j * H + h
                                if h < K:
                                    nc.tensor.matmul(
                                        neg_bank[:, lo:lo + NC],
                                        edge[c % EDGE_SLOTS][:, at:at + P].bitcast(FP8),
                                        L.v_neg[:, sweep, pair].rearrange("p k w -> p (k w)"),
                                        start=begin and h == 0, stop=False, skip_group_check=True)
                                nc.tensor.matmul(
                                    pos_bank[:, column_of(h, 0):column_of(h, 0) + PC],
                                    pos[m][:, h, at:at + P].bitcast(FP8),
                                    L.v_pos[:, sweep, pair, 0:PC],
                                    start=begin and h == 0 and not K, stop=end,
                                    skip_group_check=H > 1)
                                mask = pos[m][:, h] if h < K else neg[m][:, h - K]
                                values = v_sub[:, j, h] if h < K else L.v_neg[:, sweep, pair]
                                last = nc.tensor.matmul(
                                    neg_bank[:, lo:lo + NC], mask[:, at:at + P].bitcast(FP8),
                                    values.rearrange("p k w -> p (k w)"),
                                    start=begin and neg_bank is not pos_bank, stop=end,
                                    skip_group_check=H > 1)
                        if i == IT - 1:
                            last.then_inc(masks_used, 1)
                        elif c == nb - 1:
                            last.then_inc(sums_done, 1)

        @block.gpsimd
        def _(pool):
            pool.sem_inc(out_vector, BANKS // 2)
            pool.sem_inc(out_scalar, BANKS // 2)
            pool.sem_inc(sums_used, 1)
            nc.gpsimd.memset(minus_one[:, :], -1.0).then_inc(consts_ready, 1)
            nc.gpsimd.memset(minus_half[:, :], -0.5).then_inc(consts_ready, 1)
            pool.wait_ge(consts_ready, 2)
            for g in range(nb):
                pool.wait_ge(mid_ready, g + 1)
                nc.gpsimd.tensor_tensor(L.pos_part(sweep, g, 2), rest[:, 0], L.pos_part(sweep, g, 1),
                                        ALU.subtract).then_inc(last_parts, 1)

            def finish_slab(slab, y_waits):
                per_slab = 6 + 3 * first + 3 * closes
                steps = [0]

                def link(instruction):
                    steps[0] += 1
                    instruction.then_inc(pool_seq, 1)
                    stand(pool.wait_ge(pool_seq, slab * per_slab + steps[0]), passed["pool"])

                factor = [a[:, sweep, :, :].rearrange("p t h -> p (t h)")
                          [:, bass.ds(slab * G, G)].unsqueeze(2).broadcast_to([P, G, W])
                          for a in (L.alpha, L.beta)]
                flat = [a[:, :, :, :].rearrange("p i h w -> p (i h) w") for a in acc]
                for out in (out_vector, out_scalar):
                    stand(pool.wait_ge(out, slab * (BANKS // 2) + BANKS), passed["pool"])
                if y_waits and not closes:
                    stand(pool.wait_ge(y_ready, slab), passed["pool"])
                nc.gpsimd.tensor_tensor(acc[0][:, :, :, :], sums[:, :, :, 1, :],
                                        sums[:, :, :, 2, :], ALU.add)
                link(nc.gpsimd.tensor_tensor(acc[1][:, :, :, :], sums[:, :, :, POS_PARTS, :],
                                             sums[:, :, :, POS_PARTS + 1, :], ALU.add))
                link(nc.gpsimd.tensor_tensor(acc[0][:, :, :, :], acc[0][:, :, :, :],
                                             sums[:, :, :, 0, :], ALU.add))
                pool.sem_inc(sums_used, 1)
                nc.gpsimd.tensor_tensor(flat[1], flat[1], factor[1], ALU.mult)
                link(nc.gpsimd.tensor_tensor(flat[0], flat[0], factor[0], ALU.mult))
                link(nc.gpsimd.tensor_tensor(flat[0], flat[0], flat[1], ALU.add))
                if first:
                    link(nc.gpsimd.tensor_scalar(lone[:, :], flat[0][:, :, W - 1], 0.0, None,
                                                 ALU.is_equal))
                    link(nc.gpsimd.tensor_tensor(flat[1], lone[:, :].unsqueeze(2)
                                                 .broadcast_to([P, G, W]),
                                                 L.all_sum[:, :].unsqueeze(1)
                                                 .broadcast_to([P, G, W]), ALU.mult))
                    link(nc.gpsimd.tensor_tensor(flat[0], flat[0], flat[1], ALU.add))
                link(nc.gpsimd.tensor_tensor(inv[:, :], flat[0][:, :, W - 1], minus_one[:, :],
                                             ALU.pow))
                link(nc.gpsimd.tensor_tensor(flat[1][:, :, 0:W - 1], flat[0][:, :, 0:W - 1],
                                             inv[:, :].unsqueeze(2).broadcast_to([P, G, W - 1]),
                                             ALU.mult))
                x_dmas = len(residual)
                stand(pool.wait_ge(x_in, slab * (16 * x_dmas) + 16 * x_dmas), passed["pool"])
                heads = lambda a: a[:, :, cols].rearrange("p i (h w) -> p i h w", h=H)
                if not closes:
                    if y_waits:
                        stand(pool.wait_ge(y_stored, slab * 16), passed["pool"])
                    nc.gpsimd.tensor_tensor(heads(y_sb), acc[1][:, :, :, 0:W - 1], heads(x_sb),
                                            ALU.add).then_inc(y_ready, 1)
                    return
                nc.gpsimd.tensor_tensor(heads(x_sb), acc[1][:, :, :, 0:W - 1], heads(x_sb),
                                        ALU.add).then_inc(res_ready, 1)
                stand(pool.wait_ge(moments_ready, slab + 1), passed["pool"])
                link(nc.gpsimd.tensor_scalar(rstd[:, :], moments[:, :, 1], EPS, None, ALU.add))
                link(nc.gpsimd.tensor_tensor(rstd[:, :], rstd[:, :], minus_half[:, :], ALU.pow))
                if y_waits:
                    stand(pool.wait_ge(y_stored, slab * 16), passed["pool"])
                link(nc.gpsimd.tensor_tensor(y_sb[:, :, :], x_sb[:, :, :],
                                             moments[:, :, 0:1].broadcast_to([P, IT, P]),
                                             ALU.subtract))
                nc.gpsimd.tensor_tensor(y_sb[:, :, :], y_sb[:, :, :],
                                        rstd[:, :].unsqueeze(2).broadcast_to([P, IT, P]),
                                        ALU.mult).then_inc(y_ready, 1)

            finish_slab(0, False)
            with pool.Fori(1, slabs) as slab:
                finish_slab(slab, True)


def build(nc, adj, x, x_t, proj0, proj0_t, att0, proj1, proj1_t, att1_src, att1_dst, out):
    n = x.shape[0]
    tiles = n // P
    layers = [Layer(0, heads=1, sweeps=1, strips=1, whole=0, scalar_share=(JB,)),
              Layer(1, heads=4, sweeps=2, strips=2, whole=1, scalar_share=(5, 4, 5, 5))]
    blocks = (n // STRIP) * (tiles // JB)
    edge_bytes = nc.dram_tensor("edge_bytes", [blocks, P, JB * STRIP], I8, kind="Internal").ap()
    x1 = nc.dram_tensor("x1", [n, P], FP32, kind="Internal").ap()
    half = P // 2
    x1_half = nc.dram_tensor("x1_half", [n, half], FP32, kind="Internal").ap()
    rows = [nc.dram_tensor(f"score_rows{L.index}", [L.heads, n], FP32, kind="Internal").ap()
            for L in layers]
    att1 = [[a[h:h + 1, :].rearrange("a d -> d a") for h in range(layers[1].heads)]
            for a in (att1_src, att1_dst)]
    with ExitStack() as keep:
        passed = {e: keep.enter_context(nc.semaphore(f"passed_{e}"))
                  for e in ("act", "dve", "pe", "pool", "sp")}
        with ExitStack() as ctx:
            layers[0].allocate(nc, ctx, tiles)
            project(nc, keep, layers[0], None, x_t, proj0, proj0_t, [att0], rows[0], n)
            attend(nc, keep, layers[0], 0, adj, edge_bytes, [(x, 0)], x1, rows[0], passed, n)
        with ExitStack() as ctx:
            layers[1].allocate(nc, ctx, tiles)
            project(nc, keep, layers[1], x1, None, proj1, proj1_t, att1, rows[1], n)
            attend(nc, keep, layers[1], 0, None, edge_bytes, [(x1[:, 0:half], 0)], x1_half,
                   rows[1], passed, n)
            attend(nc, keep, layers[1], 1, None, edge_bytes,
                   [(x1_half, 0), (x1[:, half:P], half)], out, rows[1], passed, n)


def kernel(x, adj, L0_gnn_Ws, L0_gnn_a, L1_gnn_W, L1_gnn_attn_src, L1_gnn_attn_dst):
    import numpy as np
    import concourse.bacc as bacc
    from concourse.bass_utils import run_bass_kernel_spmd

    x, adj = np.asarray(x), np.asarray(adj)
    n = x.shape[0]
    tiles, strips = n // P, n // STRIP
    blocks = adj.reshape(strips, STRIP, tiles // JB, JB, P).transpose(0, 2, 4, 3, 1)
    Ws, W1 = np.asarray(L0_gnn_Ws), np.asarray(L1_gnn_W)
    arrays = {
        "adj": blocks.reshape(strips * (tiles // JB), P, JB * STRIP),
        "x": x,
        "x_t": x.T,
        "proj0": Ws,
        "proj0_t": Ws.T,
        "att0": np.asarray(L0_gnn_a).reshape(2, P).T,
        "proj1": W1.T,
        "proj1_t": W1,
        "att1_src": np.asarray(L1_gnn_attn_src)[0],
        "att1_dst": np.asarray(L1_gnn_attn_dst)[0],
    }
    arrays = {k: np.ascontiguousarray(v) for k, v in arrays.items()}
    nc = bacc.Bacc("TRN2", target_bir_lowering=False, num_devices=1)
    args = [nc.dram_tensor(k, v.shape, mybir.dt.from_np(v.dtype), kind="ExternalInput").ap()
            for k, v in arrays.items()]
    out = nc.dram_tensor("out", [n, P], FP32, kind="ExternalOutput").ap()
    build(nc, *args, out)
    return run_bass_kernel_spmd(nc, [arrays], core_ids=[0]).results[0]["out"]
```

```python
from contextlib import ExitStack

import concourse.bass as bass
from concourse import mybir

FP32, FP16 = mybir.dt.float32, mybir.dt.float16
I8, I32, FP8 = mybir.dt.int8, mybir.dt.int32, mybir.dt.float8e4
ALU = mybir.AluOpType
ACT = mybir.ActivationFunctionType
AX = mybir.AxisListType

P = 128
JB = 4
STRIP = 512
BANKS = 8
PARTS = 2
TOP = 2.0 ** 15
LIFT = 2.0 ** 12
ON = 64.0
SLOPE = 0.2
EPS = 1e-5
ADJ_SLOTS = 4
OUT_SLOTS = 4
EDGE_SLOTS = 4
MASK_SLOTS = 2
FULL_SLOTS = 2
FEAT_SLOTS = 4


class Layer:

    def __init__(self, index, heads, sweeps, strips, whole, scalar_share, opening_share):
        self.index, self.heads = index, heads
        self.sweeps = sweeps
        self.sweep_heads = heads // sweeps
        self.strips = strips
        self.slab = strips * STRIP
        self.whole = whole
        self.scalar_share = scalar_share
        self.opening_share = opening_share
        self.width = P // heads + 1
        self.part_cols = PARTS * self.width
        self.kinds = 3 if max(whole) else 2
        self.name = f"l{index}_"

    def allocate(self, nc, ctx, tiles):
        sb = lambda s, shape, dt: ctx.enter_context(nc.sbuf_tensor(self.name + s, shape, dt))
        S, H, W = self.sweeps, self.sweep_heads, self.width
        self.values = sb("values", [P, S, tiles * H, self.kinds * self.part_cols], FP16)
        self.t_neg = sb("t_neg", [P, S, tiles, H], FP32)
        self.factors = sb("factors", [P, S, tiles, H, 2], FP32)
        self.wgt = sb("wgt", [P, 2, S, tiles, H], FP32)
        self.all_sum = sb("all_sum", [P, W], FP32) if self.index == 0 else None

    def group(self, g):
        return slice(g * JB * self.sweep_heads, (g + 1) * JB * self.sweep_heads)

    def kept(self, s, g):
        return self.values[:, s, self.group(g), 0:2 * (self.width - 1)].bitcast(FP32)

    def parts(self, s, g, q):
        return self.by_kind(s, g, q)[:, ::self.kinds - 1]

    def minus_parts(self, s, g, q):
        return self.by_kind(s, g, q)[:, 1]

    def by_kind(self, s, g, q):
        return (self.values[:, s, self.group(g), :]
                .rearrange("p g (k q w) -> p k g q w", q=PARTS, w=self.width)[:, :, :, q, :])


def stand(wait, passed):
    wait.then_inc(passed, 1)


def chain(eng, sem):
    count = [0]

    def link(instruction):
        count[0] += 1
        instruction.then_inc(sem, 1)
        eng.wait_ge(sem, count[0])

    return link


def project(nc, keep, L, x_dram, feat_t_dram, proj, proj_t, att, score_row_dram, n):
    H, W = L.heads, L.width
    tiles = n // P
    groups = tiles // JB
    gw = JB * P
    name = L.name
    S, SH = L.sweeps, L.sweep_heads
    pairs = H * tiles
    rb = min(P, pairs)
    row_blocks = pairs // rb
    transposed = x_dram is None
    with ExitStack() as ctx:
        sb = lambda s, shape, dt: ctx.enter_context(nc.sbuf_tensor(name + s, shape, dt))
        pb = lambda s, shape, dt: ctx.enter_context(nc.psum_tensor(name + s, shape, dt))
        sem = lambda s: keep.enter_context(nc.semaphore(name + s))

        feat_t = sb("feat_t", [P, n], FP32)
        feat = None if transposed else sb("feat", [P, FEAT_SLOTS, JB, P], FP32)
        ident = sb("ident", [P, P], FP32)
        proj_sb = sb("proj_sb", [P, P + 2 * H], FP32)
        proj_t_sb = sb("proj_t_sb", [P, P], FP32)
        att_sb = sb("att_sb", [P, 2 * H], FP32)
        scores = sb("scores", [P, 2 * H, tiles], FP32)
        row_sb = sb("row_sb", [P, row_blocks, P], FP32)
        val_max = sb("val_max", [P, S * groups], FP32)
        pmax = sb("pmax", [P, H + 1], FP32)
        gmax = sb("gmax", [P, H + 1], FP32)
        up = sb("up", [P, 1], FP32)
        z_t = sb("z_t", [P, S, tiles, SH], FP32)
        z_e = sb("z_e", [P, S, tiles, SH], FP32)
        z_s = sb("z_s", [P, S, tiles, SH], FP32)
        z_alpha = sb("z_alpha", [P, S, tiles, SH], FP32)
        z_beta = sb("z_beta", [P, S, tiles, SH], FP32)
        part_sum = sb("part_sum", [P, groups], FP32)
        feat_sum = sb("feat_sum", [P, 1], FP32)
        feat_sums = sb("feat_sums", [P, P], FP32)

        tr_ps = [pb(f"tr_ps{i}", [P, gw], FP32) for i in range(2)]
        val_ps = [pb(f"val_ps{i}", [P, JB, 256], FP32) for i in range(2)]
        row_ps = pb("row_ps", [P, row_blocks, P], FP32)
        small_ps = pb("small_ps", [P, 2 * H + P], FP32)
        watt_ps, sum_ps = small_ps[:, 0:2 * H], small_ps[:, 2 * H:]

        weights_in, att_ready = sem("weights_in"), sem("att_ready")
        feat_in = [sem(f"feat_in{i}") for i in range(groups // 2 if transposed else FEAT_SLOTS)]
        ident_zero, ident_ready = sem("ident_zero"), sem("ident_ready")
        watt_done, watt_ready = sem("watt_done"), sem("watt_ready")
        tr_done, feat_t_ready = sem("tr_done"), sem("feat_t_ready")
        val_done, val_kept, val_max_ready = sem("val_done"), sem("val_kept"), sem("val_max_ready")
        scores_ready = sem("scores_ready")
        rows_done, rows_ready, rows_stored = sem("rows_done"), sem("rows_ready"), sem("rows_stored")
        pmax_ready, gmax_ready = sem("pmax_ready"), sem("gmax_ready")
        z_ready, expo_done, dve_seq = sem("z_ready"), sem("expo_done"), sem("dve_seq")
        feat_sums_ready, all_sum_done = sem("feat_sums_ready"), sem("all_sum_done")

        n_weights = 2 if H == 1 else 2 + 2 * H
        block = ctx.enter_context(nc.Block())

        @block.sync
        def _(sp):
            def load_feat(g):
                sp.dma_start(feat[:, g % FEAT_SLOTS],
                             x_dram[g * gw:(g + 1) * gw, :].rearrange("(t p) d -> p t d", p=P)
                             ).then_inc(feat_in[g % FEAT_SLOTS], 16)

            sp.dma_start(proj_sb[:, 0:P], proj).then_inc(weights_in, 16)
            sp.dma_start(proj_t_sb[:, :], proj_t).then_inc(weights_in, 16)
            if H == 1:
                sp.dma_start(att_sb[:, :], att[0]).then_inc(att_ready, 16)
            else:
                sp.wait_ge(att_ready, 1)
                for k in range(2):
                    for h in range(H):
                        d = P // H
                        sp.dma_start(att_sb[h * d:(h + 1) * d, k * H + h:k * H + h + 1],
                                     att[k][h]).then_inc(weights_in, 16)
            if transposed:
                for g in range(0, groups, 2):
                    sp.dma_start(feat_t[:, g * gw:(g + 2) * gw],
                                 feat_t_dram[:, g * gw:(g + 2) * gw]).then_inc(feat_in[g // 2], 16)
            else:
                for g in range(FEAT_SLOTS):
                    load_feat(g)
            if not transposed:
                for g in range(FEAT_SLOTS, groups):
                    sp.wait_ge(tr_done, g - FEAT_SLOTS + 1)
                    load_feat(g)
            row_pairs = score_row_dram.rearrange("h (t p) -> (h t) p", p=P)
            for r in range(row_blocks):
                sp.wait_ge(rows_ready, 1)
                sp.dma_start(row_pairs[r * rb:(r + 1) * rb, :],
                             row_sb[0:rb, r, :]).then_inc(rows_stored, 16)
            sp.wait_ge(rows_stored, 16 * row_blocks)

        @block.gpsimd
        def _(pool):
            nc.gpsimd.memset(ident[:, :], 0.0).then_inc(ident_zero, 1)
            pool.wait_ge(ident_zero, 1)
            nc.gpsimd.affine_select(out=ident[:, :], in_=ident[:, :], compare_op=ALU.not_equal,
                                    fill=1.0, base=0, pattern=[[-1, P]],
                                    channel_multiplier=1).then_inc(ident_ready, 1)
            pool.wait_ge(pmax_ready, 2)
            nc.gpsimd.partition_all_reduce(gmax[:, :], pmax[:, :], P,
                                           bass.bass_isa.ReduceOp.max).then_inc(gmax_ready, 1)

        @block.tensor
        def _(pe):
            def transpose(g):
                pe.wait_ge(feat_in[g % FEAT_SLOTS], 16 * (g // FEAT_SLOTS + 1))
                if g >= 2:
                    pe.wait_ge(feat_t_ready, g - 1)
                for t in range(JB):
                    last = nc.tensor.transpose(tr_ps[g % 2][:, t * P:(t + 1) * P],
                                               feat[:, g % FEAT_SLOTS, t, :], ident[:, :])
                last.then_inc(tr_done, 1)

            pe.wait_ge(weights_in, 16 * n_weights)
            if H == 1:
                pe.wait_ge(att_ready, 16)
            nc.tensor.matmul(watt_ps, proj_t_sb[:, :], att_sb[:, :], start=True,
                             stop=True).then_inc(watt_done, 1)
            pe.wait_ge(ident_ready, 1)
            if not transposed:
                transpose(0)
            pe.wait_ge(watt_ready, 1)
            for g in range(groups):
                if transposed:
                    pe.wait_ge(feat_in[g // 2], 16)
                else:
                    if g + 1 < groups:
                        transpose(g + 1)
                    pe.wait_ge(feat_t_ready, g + 1)
                if g >= 2:
                    pe.wait_ge(scores_ready, g - 1)
                for t in range(JB):
                    last = nc.tensor.matmul(val_ps[g % 2][:, t, 0:P + 2 * H],
                                            feat_t[:, (g * JB + t) * P:(g * JB + t + 1) * P],
                                            proj_sb[:, :], start=True, stop=True)
                last.then_inc(val_done, 1)
            pe.wait_ge(scores_ready, groups)
            s_flat = scores[:, 0:H, :].rearrange("p h t -> p (h t)")
            for r in range(row_blocks):
                last = nc.tensor.transpose(row_ps[0:rb, r, :], s_flat[:, r * rb:(r + 1) * rb],
                                           ident[:, :])
            last.then_inc(rows_done, 1)
            if L.all_sum is not None:
                pe.wait_ge(feat_sums_ready, 1)
                nc.tensor.matmul(sum_ps, feat_sums[:, :], proj_sb[:, 0:P], start=True,
                                 stop=True).then_inc(all_sum_done, 1)

        @block.scalar
        def _(act):
            for g in range(groups):
                act.wait_ge(val_done, g + 1)
                by_sweep = val_ps[g % 2][:, :, 0:P].rearrange("p t (s h w) -> p s t h w", s=S, h=SH)
                for s in range(S):
                    last = nc.scalar.activation(
                        L.kept(s, g).rearrange("p (t h) w -> p t h w", h=SH), by_sweep[:, s],
                        ACT.Copy)
                last.then_inc(val_kept, 1)
                last = nc.scalar.activation(
                    scores[:, :, g * JB:(g + 1) * JB].rearrange("p c t -> p t c"),
                    val_ps[g % 2][:, :, P:P + 2 * H], ACT.Copy)
                last.then_inc(scores_ready, 1)
            act.wait_ge(rows_done, 1)
            nc.scalar.activation(row_sb[0:rb, :, :], row_ps[0:rb, :, :],
                                 ACT.Copy).then_inc(rows_ready, 1)
            act.wait_ge(z_ready, 1)
            nc.scalar.activation(z_e[:, :, :, :], z_t[:, :, :, :], ACT.Exp)
            nc.scalar.activation(z_t[:, :, :, :], z_t[:, :, :, :], ACT.Exp,
                                 scale=SLOPE).then_inc(expo_done, 1)
            act.wait_ge(z_ready, 2)
            nc.scalar.activation(L.factors[:, :, :, :, 0], z_alpha[:, :, :, :], ACT.Exp)
            nc.scalar.activation(L.factors[:, :, :, :, 1], z_beta[:, :, :, :], ACT.Exp)

        @block.vector
        def _(dve):
            link = chain(dve, dve_seq)
            if H > 1:
                nc.vector.memset(att_sb[:, :], 0.0).then_inc(att_ready, 1)
            dve.wait_ge(watt_done, 1)
            nc.vector.tensor_copy(proj_sb[:, P:], watt_ps).then_inc(watt_ready, 1)

            def copy_feat(g):
                dve.wait_ge(tr_done, g + 1)
                nc.vector.tensor_copy(feat_t[:, g * gw:(g + 1) * gw],
                                      tr_ps[g % 2][:, :]).then_inc(feat_t_ready, 1)

            if not transposed:
                copy_feat(0)
            for g in range(groups):
                if not transposed and g + 1 < groups:
                    copy_feat(g + 1)
                if L.all_sum is not None:
                    dve.wait_ge(feat_in[g // 2], 16)
                    nc.vector.reduce_sum(part_sum[:, g:g + 1], feat_t[:, g * gw:(g + 1) * gw],
                                         axis=AX.X)
                dve.wait_ge(val_kept, g + 1)
                for s in range(S):
                    nc.vector.tensor_reduce(val_max[:, s * groups + g:s * groups + g + 1],
                                            L.kept(s, g), AX.XY, ALU.max,
                                            apply_absolute_value=True).then_inc(val_max_ready, 1)
            dve.wait_ge(scores_ready, groups)
            s_cols = scores[:, 0:H, :].rearrange("p (s h) t -> p s t h", s=S)
            t_cols = scores[:, H:2 * H, :].rearrange("p (s h) t -> p s t h", s=S)
            nc.vector.tensor_reduce(pmax[:, 0:H], scores[:, H:2 * H, :], AX.X,
                                    ALU.max).then_inc(pmax_ready, 1)
            dve.wait_ge(val_max_ready, S * groups)
            link(nc.vector.tensor_reduce(up[:, :], val_max[:, :], AX.X, ALU.max))
            nc.vector.tensor_scalar(pmax[:, H:H + 1], up[:, :], 1.0, None,
                                    ALU.max).then_inc(pmax_ready, 1)
            link(nc.vector.tensor_scalar(L.t_neg[:, :, :, :], t_cols, -1.0, None, ALU.mult))
            if L.all_sum is not None:
                link(nc.vector.reduce_sum(feat_sum[:, :], part_sum[:, :], axis=AX.X))
                nc.vector.tensor_copy(feat_sums[:, :],
                                      feat_sum[:, :].broadcast_to([P, P])
                                      ).then_inc(feat_sums_ready, 1)
            top = (gmax[:, 0:H].rearrange("p (s h) -> p s h", s=S).unsqueeze(2)
                   .broadcast_to([P, S, tiles, SH]))
            dve.wait_ge(gmax_ready, 1)
            nc.vector.tensor_tensor(z_t[:, :, :, :], t_cols, top, ALU.subtract).then_inc(z_ready, 1)
            link(nc.vector.tensor_tensor(z_s[:, :, :, :], s_cols, top, ALU.add))
            nc.vector.tensor_scalar(z_alpha[:, :, :, :], z_s[:, :, :, :], 1.0 - SLOPE, 0.0,
                                    ALU.mult, ALU.min)
            nc.vector.tensor_scalar(z_beta[:, :, :, :], z_s[:, :, :, :], SLOPE - 1.0, 0.0,
                                    ALU.mult, ALU.min).then_inc(z_ready, 1)
            link(nc.vector.tensor_scalar(up[:, :], gmax[:, H:H + 1], 1.0 / TOP, None, ALU.mult))
            link(nc.vector.reciprocal(up[:, :], up[:, :]))
            dve.wait_ge(expo_done, 1)
            nc.vector.tensor_scalar(L.wgt[:, 0], z_e[:, :, :, :], up[:, :], None, ALU.mult)
            nc.vector.tensor_scalar(L.wgt[:, 1], z_t[:, :, :, :], up[:, :], None, ALU.mult)
            if L.all_sum is not None:
                nc.vector.memset(L.all_sum[:, W - 1:W], float(n))
                dve.wait_ge(all_sum_done, 1)
                nc.vector.tensor_copy(L.all_sum[:, 0:W - 1], sum_ps)


class Pass:

    def __init__(self, L, slabs, sweep, slab):
        self.L, self.slabs, self.sweep, self.slab = L, slabs, sweep, slab
        self.before = slab + sweep * slabs
        fixed = isinstance(slab, int)
        self.opening = fixed and slab == 0
        self.very_first = self.opening and sweep == 0
        self.ends_sweep = fixed and slab == slabs - 1
        self.closes = sweep == L.sweeps - 1
        self.final = self.closes and self.ends_sweep

    def at(self, sweep, slab):
        return Pass(self.L, self.slabs, sweep, slab)

    def next(self):
        return self.at(self.sweep + 1, 0) if self.ends_sweep else self.at(self.sweep, self.slab + 1)

    def previous(self):
        if self.opening:
            return self.at(self.sweep - 1, self.slabs - 1)
        return self.at(self.sweep, self.slab - 1)


def attend(nc, keep, L, adj, edge_bytes, residuals, outs, score_row_dram, passed, n):
    H, W, C = L.sweep_heads, L.width, L.part_cols
    tiles = n // P
    slabs = n // L.slab
    rows = L.slab
    IT = rows // P
    nb = tiles // JB
    ahead = max(2, nb * 5 // 8)
    store_at = nb * 3 // 4
    words = JB * rows // 4
    first = L.index == 0
    S = L.sweeps
    name = L.name
    G = IT * H
    K = lambda c: L.whole[c % len(L.whole)]
    chained = [4 + 3 * first + 3 * (s == S - 1) for s in range(S)]
    x_counts = [16 * len(r) for r in residuals]
    with ExitStack() as ctx:
        sb = lambda s, shape, dt: ctx.enter_context(nc.sbuf_tensor(name + s, shape, dt))
        sem = lambda s: keep.enter_context(nc.semaphore(name + s))

        s_rows = sb("s_rows", [P, 2 * H * rows], FP32)
        above = [sb(f"above{i}", [P, H, JB * rows], I8) for i in range(MASK_SLOTS)]
        pos = [sb(f"pos{i}", [P, H, JB * rows], I8) for i in range(MASK_SLOTS)]
        neg = [sb(f"neg{i}", [P, H - min(L.whole), JB * rows], I8) for i in range(MASK_SLOTS)]
        if first:
            adj_sb = [sb(f"adj_sb{i}", [P, JB * rows], I32) for i in range(ADJ_SLOTS)]
            edge = [sb(f"edge{i}", [P, JB * rows], I8) for i in range(MASK_SLOTS)]
            next_edge = [sb(f"next_edge{i}", [P, JB * rows], I8) for i in range(OUT_SLOTS)]
        else:
            edge = [sb(f"edge{i}", [P, JB * rows], I8) for i in range(EDGE_SLOTS)]
        full = [sb(f"full{i}", [P, 2, JB * H, W], FP32)
                for i in range(FULL_SLOTS)]
        rest = sb("rest", [P, 2, JB * H, W], FP32)
        sums = sb("sums", [P, G, 2, W], FP32)
        low = sb("low", [P, G, 2, W], FP32)
        acc = sb("acc", [P, G, 2, W], FP32)
        x_sb = sb("x_sb", [P, IT, P], FP32)
        y_sb = sb("y_sb", [P, IT, P], FP32)
        inv = sb("inv", [P, G], FP32)
        minus_one = sb("minus_one", [P, G], FP32)
        minus_half = sb("minus_half", [P, IT], FP32)
        stats = sb("stats", [P, IT, 6], FP32)
        moments = sb("moments", [P, IT, 2], FP32)
        rstd = sb("rstd", [P, IT], FP32)
        lone = sb("lone", [P, G], FP32)
        banks = [ctx.enter_context(nc.psum_tensor(f"{name}bank{i}", [P, 512], FP32))
                 for i in range(BANKS)]

        def bank_of(i, negative):
            return 2 * i + negative if IT * 2 == BANKS else i

        def column_of(h, negative):
            return h * C if IT * 2 == BANKS else (h * 2 + negative) * C

        def sums_of(b):
            if IT * 2 == BANKS:
                i, negative = divmod(b, 2)
                branches = slice(negative, negative + 1)
            else:
                i, branches = b, slice(0, 2)
            k = branches.stop - branches.start
            filled = banks[b][:, 0:H * k * C]
            return (filled.rearrange("p (h k q w) -> p q h k w", k=k, q=PARTS, w=W),
                    i, (slice(None), slice(i * H, (i + 1) * H), branches))

        block_in = [sem(f"block_in{i}") for i in range(max(ADJ_SLOTS, EDGE_SLOTS))]
        if first:
            edge_stored = [sem(f"edge_stored{i}") for i in range(OUT_SLOTS)]
            edge_ready = sem("edge_ready")
            next_edge_ready = sem("next_edge_ready")
        rows_in = sem("rows_in")
        above_scalar = sem("above_scalar")
        above_vector = sem("above_vector")
        pos_ready = sem("pos_ready")
        neg_ready = sem("neg_ready")
        masks_used = sem("masks_used")
        sums_done = sem("sums_done")
        low_out = sem("low_out")
        banks_out = sem("banks_out")
        sums_used = sem("sums_used")
        x_in, y_ready, y_stored = sem("x_in"), sem("y_ready"), sem("y_stored")
        res_ready, stats_ready, moments_ready, scale_ready = (
            sem("res_ready"), sem("stats_ready"), sem("moments_ready"), sem("scale_ready"))
        pool_seq, tail_seq, consts_ready = sem("pool_seq"), sem("tail_seq"), sem("consts_ready")
        full_ready, first_ready, rest_ready, second_ready = (
            sem("full_ready"), sem("first_ready"), sem("rest_ready"), sem("second_ready"))

        block = ctx.enter_context(nc.Block())

        def each_pass(eng, work):
            for sweep in range(S):
                work(Pass(L, slabs, sweep, 0))
                with eng.Fori(1, slabs - 1) as slab:
                    work(Pass(L, slabs, sweep, slab))
                work(Pass(L, slabs, sweep, slabs - 1))

        def split_group(p, c):
            if p.opening and c < nb:
                return p.sweep, c
            if p.ends_sweep and not p.final and c >= nb:
                return p.sweep + 1, c - nb
            return None

        def first_masks(p, blocks):
            return p.before * (nb * H) + blocks * H

        def seconds(c):
            return sum(K(b) < H for b in range(c + 1))

        @block.sync
        def _(sp):
            n_slots = ADJ_SLOTS if first else EDGE_SLOTS
            slot_sb = adj_sb if first else edge
            src = adj if first else edge_bytes
            src_blocks = src.rearrange("(s k c) p n -> s c p k n", k=L.strips, c=nb)

            def load(p, c):
                slab = p.slab if c < nb else p.next().slab
                sp.dma_start(slot_sb[c % n_slots][:, :].rearrange("p (k n) -> p k n", k=L.strips),
                             src_blocks[bass.ds(slab, 1), c % nb, :, :, :]
                             .rearrange("a p k n -> (a p) k n")).then_inc(block_in[c % n_slots], 16)

            def load_rows(p):
                for h in range(H):
                    sp.dma_start(s_rows[:, bass.ds((p.slab % 2) * (H * rows) + h * rows, rows)],
                                 score_row_dram[p.sweep * H + h:p.sweep * H + h + 1,
                                                bass.ds(p.slab * rows, rows)]
                                 .partition_broadcast(P).rearrange("p a n -> p (a n)")
                                 ).then_inc(rows_in, 16)

            def row_tiles(dram, slab):
                return dram[bass.ds(slab * rows, rows), :].rearrange("(t p) d -> p t d", p=P)

            def load_residual(p):
                for dram, at in residuals[p.sweep]:
                    sp.dma_start(x_sb[:, :, at:at + dram.shape[1]],
                                 row_tiles(dram, p.slab)).then_inc(x_in, 16)

            def store(p):
                out = outs[p.sweep]
                stand(sp.wait_ge(y_ready, p.before + 1), passed["sp"])
                sp.dma_start(row_tiles(out, p.slab),
                             y_sb[:, :, 0:out.shape[1]]).then_inc(y_stored, 16)

            def pass_loads(p):
                for c in range(nb):
                    if first:
                        stand(sp.wait_ge(next_edge_ready, p.before * nb + (c + 1)), passed["sp"])
                        sp.dma_start(edge_bytes[bass.ds(p.slab * nb + c, 1), :, :]
                                     .rearrange("a p n -> (a p) n"), next_edge[c % OUT_SLOTS][:, :]
                                     ).then_inc(edge_stored[c % OUT_SLOTS], 16)
                    else:
                        stand(sp.wait_ge(masks_used, p.before * nb + (c + 1 + MASK_SLOTS)),
                              passed["sp"])
                    if not p.final or c + n_slots < nb:
                        load(p, c + n_slots)
                    if c == nb // 2 and not p.final:
                        stand(sp.wait_ge(pos_ready, first_masks(p, 1 + MASK_SLOTS)), passed["sp"])
                        load_rows(p.next())
                    if c == store_at and not p.very_first:
                        store(p.previous())
                        load_residual(p)

            begin = Pass(L, slabs, 0, 0)
            load_rows(begin)
            for c in range(n_slots):
                load(begin, c)
            load_residual(begin)
            each_pass(sp, pass_loads)
            store(Pass(L, slabs, S - 1, slabs - 1))
            sp.wait_ge(y_stored, 16 * slabs * S)
            if first:
                for i in range(OUT_SLOTS):
                    sp.wait_ge(edge_stored[i], 16 * (slabs * nb // OUT_SLOTS + 1))

        def above_row(p, c, h):
            return (s_rows[:, bass.ds(((p.slab + c // nb) % 2) * (H * rows) + h * rows, rows)]
                    .rearrange("p (k r) -> p k r", r=STRIP))

        def above_part(m, h, t):
            return above[m][:, h, :].rearrange("p (k t r) -> p k t r", t=JB, r=STRIP)[:, :, t, :]

        def t_of(p, c, t, h):
            sweep = p.next().sweep if c >= nb else p.sweep
            return L.t_neg[:, sweep, (c % nb) * JB + t, h:h + 1]

        def comparisons(p, c, scalar):
            splits = split_group(p, c) or split_group(p, c - 1)
            shares, total = L.opening_share if splits else L.scalar_share, H * JB
            share = shares[c % len(shares)]
            mine = [divmod(k, JB) for k in range(total)
                    if ((k + 1) * share // total > k * share // total) == scalar]
            return sorted(mine, key=lambda pair: (-pair[0], pair[1]))

        def head_done(mine, k):
            return k == len(mine) - 1 or mine[k + 1][0] != mine[k][0]

        def banks_between(k, n):
            return k * BANKS // n, (k + 1) * BANKS // n

        def row_tile_done(eng, p, i):
            if i < IT - 1:
                return eng.wait_ge(sums_done, p.before * (IT - 1) + (i + 1))
            return eng.wait_ge(masks_used, p.before * nb + (nb + MASK_SLOTS))

        def row_moments(dve, p):
            dve.wait_ge(res_ready, p.slab + 1)
            for i in range(IT):
                last = nc.vector.bn_stats(stats[:, i, :], x_sb[:, i, :])
            last.then_inc(stats_ready, 1)
            stand(dve.wait_ge(stats_ready, p.slab + 1), passed["dve"])
            for i in range(IT):
                last = nc.vector.bn_aggr(moments[:, i, :], stats[:, i, :])
            last.then_inc(moments_ready, 1)

        def row_scale(pool, link, p):
            stand(pool.wait_ge(moments_ready, p.slab + 1), passed["pool"])
            link(nc.gpsimd.tensor_scalar(rstd[:, :], moments[:, :, 1], EPS, None, ALU.add))
            link(nc.gpsimd.tensor_tensor(rstd[:, :], rstd[:, :], minus_half[:, :], ALU.pow))
            pool.sem_inc(scale_ready, 1)

        def finish(eng, math, who, seq, done, p):
            steps = [0]

            def link(instruction):
                steps[0] += 1
                instruction.then_inc(seq, 1)
                stand(eng.wait_ge(seq, done + steps[0]), passed[who])

            factor = (L.factors[:, p.sweep, :, :, :].rearrange("p t h b -> p (t h) b")
                      [:, bass.ds(p.slab * G, G), :].unsqueeze(3).broadcast_to([P, G, 2, W]))
            total, spare = acc[:, :, 0, :], acc[:, :, 1, :]
            stand(eng.wait_ge(banks_out, p.before * BANKS + 2 * BANKS), passed[who])
            if not p.very_first and (p.final or p.opening or not p.closes):
                stand(eng.wait_ge(y_ready, p.before), passed[who])
            link(math.tensor_tensor(acc[:, :, :, :], sums[:, :, :, :], factor, ALU.mult))
            eng.sem_inc(sums_used, 1)
            link(math.tensor_tensor(total, total, spare, ALU.add))
            if first:
                link(math.tensor_scalar(lone[:, :], acc[:, :, 0, W - 1], 0.0, None,
                                        ALU.is_equal))
                link(math.tensor_tensor(spare, lone[:, :].unsqueeze(2).broadcast_to([P, G, W]),
                                        L.all_sum[:, :].unsqueeze(1).broadcast_to([P, G, W]),
                                        ALU.mult))
                link(math.tensor_tensor(total, total, spare, ALU.add))
            if p.final:
                link(math.reciprocal(inv[:, :], acc[:, :, 0, W - 1]))
            else:
                link(math.tensor_tensor(inv[:, :], acc[:, :, 0, W - 1], minus_one[:, :], ALU.pow))
            link(math.tensor_tensor(spare[:, :, 0:W - 1], total[:, :, 0:W - 1],
                                    inv[:, :].unsqueeze(2).broadcast_to([P, G, W - 1]),
                                    ALU.mult))
            attended = acc[:, :, 1, 0:W - 1].rearrange("p (i h) w -> p i h w", h=H)
            stand(eng.wait_ge(x_in, p.slab * x_counts[p.sweep]
                              + (slabs * sum(x_counts[:p.sweep]) + x_counts[p.sweep])), passed[who])
            begin = p.sweep * H * (W - 1) if p.closes else 0
            heads = lambda a: (a[:, :, begin:begin + H * (W - 1)]
                               .rearrange("p i (h w) -> p i h w", h=H))
            if not p.closes:
                if not p.very_first:
                    stand(eng.wait_ge(y_stored, p.before * 16), passed[who])
                math.tensor_tensor(heads(y_sb), attended, heads(x_sb), ALU.add).then_inc(y_ready, 1)
                return
            math.tensor_tensor(heads(x_sb), attended, heads(x_sb), ALU.add).then_inc(res_ready, 1)
            if p.final:
                row_moments(eng, p)
                eng.wait_ge(scale_ready, slabs)
            else:
                row_scale(eng, link, p)
            if not p.very_first:
                stand(eng.wait_ge(y_stored, p.before * 16), passed[who])
            link(math.tensor_tensor(y_sb[:, :, :], x_sb[:, :, :],
                                    moments[:, :, 0:1].broadcast_to([P, IT, P]),
                                    ALU.subtract))
            math.tensor_tensor(y_sb[:, :, :], y_sb[:, :, :],
                                    rstd[:, :].unsqueeze(2).broadcast_to([P, IT, P]),
                                    ALU.mult).then_inc(y_ready, 1)

        @block.scalar
        def _(act):
            def above_block(p, c, between=None):
                m, mine = c % MASK_SLOTS, comparisons(p, c, True)
                if c % nb == 0:
                    stand(act.wait_ge(rows_in, p.before * (16 * H) + (c // nb + 1) * (16 * H)),
                          passed["act"])
                stand(act.wait_ge(pos_ready, first_masks(p, c + 1)), passed["act"])
                for k, (h, t) in enumerate(mine):
                    last = nc.scalar.activation(above_part(m, h, t), above_row(p, c, h), ACT.Sign,
                                                bias=t_of(p, c, t, h), scale=-1.0)
                    if head_done(mine, k):
                        last.then_inc(above_scalar, 1)
                    if between:
                        between(p, *banks_between(k, len(mine)))

            def first_parts(sweep, g):
                act.wait_ge(full_ready, sweep * nb + g + 1)
                whole = full[g % FULL_SLOTS]
                last = nc.scalar.activation(L.parts(sweep, g, 0), whole[:, :], ACT.Copy)
                if L.kinds == 3:
                    last = nc.scalar.activation(L.minus_parts(sweep, g, 0), whole[:, 1], ACT.Copy,
                                                scale=-1.0)
                last.then_inc(first_ready, 1)

            def second_parts(sweep, g):
                act.wait_ge(rest_ready, sweep * nb + g + 1)
                last = nc.scalar.activation(L.parts(sweep, g, 1), rest[:, :], ACT.Copy, scale=LIFT)
                if L.kinds == 3:
                    last = nc.scalar.activation(L.minus_parts(sweep, g, 1), rest[:, 1], ACT.Copy,
                                                scale=-LIFT)
                last.then_inc(second_ready, 1)

            def take_low(p, begin=0, end=BANKS):
                for b in range(begin, end):
                    bank, i, at = sums_of(b)
                    stand(row_tile_done(act, p, i), passed["act"])
                    nc.scalar.activation(low[at], bank[:, 1], ACT.Copy,
                                         scale=1.0 / LIFT).then_inc(low_out, 1)

            def step(p, c, between=None):
                group = split_group(p, c - 1)
                if group:
                    first_parts(*group)
                above_block(p, c, between)
                if group:
                    second_parts(*group)

            def pass_work(p):
                if p.very_first:
                    first_parts(0, 0)
                    above_block(p, 0)
                    second_parts(0, 0)
                    above_block(p, 1)
                for c in range(2 if p.very_first else ahead, nb + (0 if p.final else 1)):
                    step(p, c)
                if p.final:
                    take_low(p)
                else:
                    step(p, nb + 1, take_low)
                    for c in range(nb + 2, nb + ahead):
                        step(p, c)

            each_pass(act, pass_work)

        @block.vector
        def _(dve):
            dve.sem_inc(pos_ready, MASK_SLOTS * H)
            if first:
                for i in range(OUT_SLOTS):
                    dve.sem_inc(edge_stored[i], 16)

            def masks(p, c, between=None):
                m, at = c % MASK_SLOTS, p.before * nb
                if first:
                    slot, out = c % ADJ_SLOTS, c % OUT_SLOTS
                    dve.wait_ge(block_in[slot], p.before * (16 * nb // ADJ_SLOTS)
                                + 16 * (c // ADJ_SLOTS + 1))
                    nc.vector.tensor_scalar(edge[m][:, :], adj_sb[slot][:, :], 0.0, ON, ALU.is_gt,
                                            ALU.mult).then_inc(edge_ready, 1)
                    dve.wait_ge(edge_stored[out], p.before * (16 * nb // OUT_SLOTS)
                                + 16 * (c // OUT_SLOTS + 1))
                    nc.vector.tensor_scalar(next_edge[out][:, :], adj_sb[slot][:, :], 0.0, ON,
                                            ALU.not_equal, ALU.mult).then_inc(next_edge_ready, 1)
                    dve.wait_ge(edge_ready, at + (c + 1))
                    edges = edge[m]
                else:
                    slot = c % EDGE_SLOTS
                    edges = edge[slot]
                    if c % nb == 0:
                        dve.wait_ge(rows_in, p.before * (16 * H) + (c // nb + 1) * (16 * H))
                    dve.wait_ge(pos_ready, first_masks(p, c + 1))
                    mine = comparisons(p, c, False)
                    for k, (h, t) in enumerate(mine):
                        last = nc.vector.tensor_scalar(
                            above_part(m, h, t), above_row(p, c, h), t_of(p, c, t, h), ON,
                            ALU.is_gt, ALU.mult)
                        if head_done(mine, k):
                            last.then_inc(above_vector, 1)
                        if between:
                            between(p, *banks_between(k, len(mine)))
                    dve.wait_ge(block_in[slot], p.before * (16 * nb // EDGE_SLOTS)
                                + 16 * (c // EDGE_SLOTS + 1))
                dve.wait_ge(masks_used, at + (c + 1))
                edge_words = edges[:, :].bitcast(I32)
                for k, h in enumerate(reversed(range(H))):
                    if not first:
                        dve.wait_ge(above_vector, first_masks(p, c) + (k + 1))
                    dve.wait_ge(above_scalar, first_masks(p, c) + (k + 1))
                    nc.vector.tensor_tensor(pos[m][:, h, :].bitcast(I32),
                                            above[m][:, h, :].bitcast(I32), edge_words,
                                            ALU.bitwise_and).then_inc(pos_ready, 1)
                if K(c) < H:
                    dve.wait_ge(pos_ready, first_masks(p, c + MASK_SLOTS) + (H - K(c)))
                    as_words = lambda x: (x[:, :, :].rearrange("p h w -> p (h w)").bitcast(I32)
                                          .rearrange("p (h w) -> p h w", w=words))
                    nc.vector.tensor_tensor(as_words(neg[m])[:, K(c) - min(L.whole):, :],
                                            as_words(pos[m])[:, K(c):H, :],
                                            edge_words.unsqueeze(1)
                                            .broadcast_to([P, H - K(c), words]),
                                            ALU.bitwise_xor).then_inc(neg_ready, 1)

            def leave(sweep, g):
                dve.wait_ge(first_ready, sweep * nb + g + 1)
                if sweep or g:
                    dve.wait_ge(second_ready, sweep * nb + g)
                nc.vector.tensor_tensor(rest[:, :], full[g % FULL_SLOTS][:, :],
                                        L.parts(sweep, g, 0), ALU.subtract).then_inc(rest_ready, 1)

            def take_out(p, begin=0, end=BANKS):
                if begin == 0:
                    dve.wait_ge(sums_used, p.before + 1)
                for b in range(begin, end):
                    bank, _, at = sums_of(b)
                    dve.wait_ge(low_out, p.before * BANKS + (b + 1))
                    nc.vector.tensor_tensor(sums[at], bank[:, 0], low[at],
                                            ALU.add).then_inc(banks_out, 1)

            def step(p, c, between=None):
                masks(p, c, between)
                group = split_group(p, c)
                if group:
                    leave(*group)

            def pass_work(p):
                if p.very_first:
                    leave(0, 0)
                    masks(p, 0)
                for c in range(1 if p.very_first else ahead, nb + (0 if p.final else 1)):
                    step(p, c)
                if p.final:
                    take_out(p)
                    finish(dve, nc.vector, "dve", tail_seq, 0, p)
                    return
                if first:
                    take_out(p)
                step(p, nb + 1, None if first else take_out)
                for c in range(nb + 2, nb + ahead):
                    step(p, c)
                if p.closes:
                    row_moments(dve, p)

            each_pass(dve, pass_work)

        @block.tensor
        def _(pe):
            pe.sem_inc(masks_used, MASK_SLOTS)
            def pass_work(p):
                for c in range(nb):
                    m = c % MASK_SLOTS
                    stand(pe.wait_ge(pos_ready, first_masks(p, c + 1 + MASK_SLOTS)),
                          passed["pe"])
                    if K(c) < H:
                        stand(pe.wait_ge(neg_ready, p.before * seconds(nb - 1) + seconds(c)),
                              passed["pe"])
                    pe.wait_ge(second_ready, p.sweep * nb + c + 1)
                    for i in range(IT):
                        if c == 0:
                            stand(pe.wait_ge(banks_out, p.before * BANKS + (bank_of(i, 1) + 1)),
                                  passed["pe"])
                        pos_bank, neg_bank = banks[bank_of(i, 0)], banks[bank_of(i, 1)]
                        for t in range(JB):
                            j = c * JB + t
                            at = (i // (STRIP // P) * JB + t) * STRIP + i % (STRIP // P) * P
                            begin, end = j == 0, j == tiles - 1
                            for h in range(H):
                                above_col, below_col = column_of(h, 0), column_of(h, 1)
                                kinds = L.values[:, p.sweep, j * H + h]
                                below = kinds[:, (L.kinds - 1) * C:L.kinds * C]
                                pos_mask = pos[m][:, h, at:at + P].bitcast(FP8)
                                if h < K(c):
                                    nc.tensor.matmul(
                                        neg_bank[:, below_col:below_col + C],
                                        edge[c % EDGE_SLOTS][:, at:at + P].bitcast(FP8), below,
                                        start=begin and h == 0, stop=False, skip_group_check=True)
                                    last = nc.tensor.matmul(
                                        pos_bank[:, above_col:above_col + 2 * C], pos_mask,
                                        kinds[:, 0:2 * C], start=False, stop=end,
                                        skip_group_check=True)
                                    continue
                                nc.tensor.matmul(
                                    pos_bank[:, above_col:above_col + C], pos_mask, kinds[:, 0:C],
                                    start=begin and h == 0, stop=end, skip_group_check=H > 1)
                                last = nc.tensor.matmul(
                                    neg_bank[:, below_col:below_col + C],
                                    neg[m][:, h - min(L.whole), at:at + P].bitcast(FP8), below,
                                    start=begin and neg_bank is not pos_bank, stop=end,
                                    skip_group_check=H > 1)
                        if i == IT - 1:
                            last.then_inc(masks_used, 1)
                        elif c == nb - 1:
                            last.then_inc(sums_done, 1)

            for sweep in range(S):
                with pe.Fori(0, slabs) as slab:
                    pass_work(Pass(L, slabs, sweep, slab))

        @block.gpsimd
        def _(pool):
            pool.sem_inc(banks_out, BANKS)
            pool.sem_inc(sums_used, 1)
            nc.gpsimd.memset(minus_one[:, :], -1.0).then_inc(consts_ready, 1)
            nc.gpsimd.memset(minus_half[:, :], -0.5).then_inc(consts_ready, 1)
            pool.wait_ge(consts_ready, 2)

            def weigh(sweep, begin, end):
                for g in range(begin, end):
                    if sweep * nb + g >= FULL_SLOTS:
                        pool.wait_ge(rest_ready, sweep * nb + g + 1 - FULL_SLOTS)
                        pool.wait_ge(first_ready, sweep * nb + g + 1 - FULL_SLOTS)
                    whole = full[g % FULL_SLOTS]
                    w = (L.wgt[:, :, sweep, g * JB:(g + 1) * JB, :]
                         .rearrange("p b t h -> p b (t h)").unsqueeze(3))
                    nc.gpsimd.tensor_tensor(whole[:, :, :, 0:W - 1],
                                            L.kept(sweep, g).unsqueeze(1)
                                            .broadcast_to([P, 2, JB * H, W - 1]),
                                            w.broadcast_to([P, 2, JB * H, W - 1]), ALU.mult)
                    nc.gpsimd.tensor_copy(whole[:, :, :, W - 1:W], w).then_inc(full_ready, 1)

            def finish_pass(p):
                done = p.slab * chained[p.sweep] + slabs * sum(chained[:p.sweep])
                finish(pool, nc.gpsimd, "pool", pool_seq, done, p)

            weighed = 0
            for sweep in range(S):
                weigh(sweep, weighed, nb)
                finish_pass(Pass(L, slabs, sweep, 0))
                with pool.Fori(1, slabs - 1) as slab:
                    finish_pass(Pass(L, slabs, sweep, slab))
                if sweep < S - 1:
                    weighed = FULL_SLOTS + 1
                    weigh(sweep + 1, 0, weighed)
                    finish_pass(Pass(L, slabs, sweep, slabs - 1))

            steps = [(slabs - 1) * chained[-1] + slabs * sum(chained[:-1])]

            def link(instruction):
                steps[0] += 1
                instruction.then_inc(pool_seq, 1)
                pool.wait_ge(pool_seq, steps[0])

            row_scale(pool, link, Pass(L, slabs, S - 1, slabs - 1))


def build(nc, adj, x, x_t, proj0, proj0_t, att0, proj1, proj1_t, att1_src, att1_dst, out):
    n = x.shape[0]
    tiles = n // P
    layers = [Layer(0, heads=1, sweeps=1, strips=1, whole=(0,), scalar_share=(JB,),
                    opening_share=(JB,)),
              Layer(1, heads=4, sweeps=2, strips=2, whole=(2, 1),
                    scalar_share=(5, 5, 5, 5, 4, 5, 5, 5), opening_share=(4,))]
    blocks = (n // STRIP) * (tiles // JB)
    edge_bytes = nc.dram_tensor("edge_bytes", [blocks, P, JB * STRIP], I8, kind="Internal").ap()
    x1 = nc.dram_tensor("x1", [n, P], FP32, kind="Internal").ap()
    half = P // 2
    x1_half = nc.dram_tensor("x1_half", [n, half], FP32, kind="Internal").ap()
    rows = [nc.dram_tensor(f"score_rows{L.index}", [L.heads, n], FP32, kind="Internal").ap()
            for L in layers]
    att1 = [[a[h:h + 1, :].rearrange("a d -> d a") for h in range(layers[1].heads)]
            for a in (att1_src, att1_dst)]
    with ExitStack() as keep:
        passed = {e: keep.enter_context(nc.semaphore(f"passed_{e}"))
                  for e in ("act", "dve", "pe", "pool", "sp")}
        with ExitStack() as ctx:
            layers[0].allocate(nc, ctx, tiles)
            project(nc, keep, layers[0], None, x_t, proj0, proj0_t, [att0], rows[0], n)
            attend(nc, keep, layers[0], adj, edge_bytes, [[(x, 0)]], [x1], rows[0], passed, n)
        with ExitStack() as ctx:
            layers[1].allocate(nc, ctx, tiles)
            project(nc, keep, layers[1], x1, None, proj1, proj1_t, att1, rows[1], n)
            attend(nc, keep, layers[1], None, edge_bytes,
                   [[(x1[:, 0:half], 0)], [(x1_half, 0), (x1[:, half:P], half)]],
                   [x1_half, out], rows[1], passed, n)


def kernel(x, adj, L0_gnn_Ws, L0_gnn_a, L1_gnn_W, L1_gnn_attn_src, L1_gnn_attn_dst):
    import numpy as np
    import concourse.bacc as bacc
    from concourse.bass_utils import run_bass_kernel_spmd

    x, adj = np.asarray(x), np.asarray(adj)
    n = x.shape[0]
    tiles, strips = n // P, n // STRIP
    blocks = adj.reshape(strips, STRIP, tiles // JB, JB, P).transpose(0, 2, 4, 3, 1)
    Ws, W1 = np.asarray(L0_gnn_Ws), np.asarray(L1_gnn_W)
    arrays = {
        "adj": blocks.reshape(strips * (tiles // JB), P, JB * STRIP),
        "x": x,
        "x_t": x.T,
        "proj0": Ws,
        "proj0_t": Ws.T,
        "att0": np.asarray(L0_gnn_a).reshape(2, P).T,
        "proj1": W1.T,
        "proj1_t": W1,
        "att1_src": np.asarray(L1_gnn_attn_src)[0],
        "att1_dst": np.asarray(L1_gnn_attn_dst)[0],
    }
    arrays = {k: np.ascontiguousarray(v) for k, v in arrays.items()}
    nc = bacc.Bacc("TRN2", target_bir_lowering=False, num_devices=1)
    args = [nc.dram_tensor(k, v.shape, mybir.dt.from_np(v.dtype), kind="ExternalInput").ap()
            for k, v in arrays.items()]
    out = nc.dram_tensor("out", [n, P], FP32, kind="ExternalOutput").ap()
    build(nc, *args, out)
    return run_bass_kernel_spmd(nc, [arrays], core_ids=[0]).results[0]["out"]
```
